# Optimizing a Trainium2 kernel written in Bass

```python
import numpy as np
import jax
import jax.numpy as jnp

def _softmax(x, axis=-1):
    return jax.nn.softmax(x, axis=axis)

def _gelu(x):
    return jax.nn.gelu(x, approximate=True)

def _silu(x):
    return jax.nn.silu(x)

def _sigmoid(x):
    return jax.nn.sigmoid(x)

def _layernorm(x, axis=-1, eps=1e-05):
    m = jnp.mean(x, axis=axis, keepdims=True)
    v = jnp.var(x, axis=axis, keepdims=True)
    return (x - m) / jnp.sqrt(v + eps)

def _scatter_add(tgt, idx, src, axis=0):
    return tgt.at[idx].add(src)

def _segment_sum(src, seg, n):
    return jax.ops.segment_sum(src, seg, n)
kernel_name = 'mk_adj_resnorm_d2_adj_r2_974245'

def setup_inputs(seed: int=0):
    np.random.seed(seed)
    _w = jnp.asarray

    def _rec_inputs():
        import jax
        import jax.numpy as jnp
        _gk = jax.random.key(seed)
        x = -0.0005207 + 1.001 * jax.random.normal(jax.random.fold_in(_gk, 1), (8192, 128), jnp.float32)
        _a = jax.random.bernoulli(jax.random.fold_in(_gk, 2), 0.000244141, (8192, 8192))
        _a = jnp.logical_or(_a, jnp.eye(8192, dtype=bool))
        _af = _a.astype(jnp.float32)
        _af = _af * jax.random.uniform(jax.random.fold_in(_gk, 3), (8192, 8192), jnp.float32, 0.05, 1)
        adj = _af
        return (x, adj)
    x, adj = _rec_inputs()

    def _L0_gnn_setup():
        import jax, jax.numpy as jnp
        import numpy as np
        ALPHA = 0.1
        N, F = (8192, 128)
        key = jax.random.key(seed)
        k1, k2, k3 = jax.random.split(key, 3)
        x = jax.random.normal(k1, (N, F), dtype=jnp.float32)
        adj = jax.random.uniform(k2, (N, N), dtype=jnp.float32)
        h = jax.random.normal(k3, (N, F), dtype=jnp.float32)
        return {'x': x, 'adj': adj, 'h': h}
    _L0_gnn_all = _L0_gnn_setup()
    _L0_gnn_in = {k: v for k, v in _L0_gnn_all.items() if k in ('h',)}
    del _L0_gnn_all

    def _L1_gnn_setup():
        import jax, jax.numpy as jnp
        import numpy as np
        N = 6144
        F_IN = 128
        F_OUT = 128
        key = jax.random.key(seed)
        k1, k2, k3, k4, k5, k6, k7 = jax.random.split(key, 7)
        stdv = 1.0 / np.sqrt(F_OUT)
        return {'feats': jax.random.normal(k1, (N, F_IN), dtype=jnp.float32), 'node_adj': jax.random.normal(k2, (N, N), dtype=jnp.float32), 'edge_adj': jax.random.normal(k3, (N, N), dtype=jnp.float32), 'node_weight': jax.random.uniform(k4, (2 * F_IN, F_OUT), dtype=jnp.float32, minval=-stdv, maxval=stdv), 'node_bias': jax.random.uniform(k5, (F_OUT,), dtype=jnp.float32, minval=-stdv, maxval=stdv), 'edge_weight': jax.random.uniform(k6, (F_IN, F_OUT), dtype=jnp.float32, minval=-stdv, maxval=stdv), 'edge_bias': jax.random.uniform(k7, (F_OUT,), dtype=jnp.float32, minval=-stdv, maxval=stdv)}
    _L1_gnn_all = _L1_gnn_setup()
    _L1_gnn_in = {k: v for k, v in _L1_gnn_all.items() if k in ('node_weight', 'node_bias', 'edge_weight', 'edge_bias')}
    del _L1_gnn_all
    return {'x': x, 'adj': adj, 'L0_gnn_h': _L0_gnn_in['h'], 'L1_gnn_node_weight': _L1_gnn_in['node_weight'], 'L1_gnn_node_bias': _L1_gnn_in['node_bias'], 'L1_gnn_edge_weight': _L1_gnn_in['edge_weight'], 'L1_gnn_edge_bias': _L1_gnn_in['edge_bias']}

def reference(x, adj, L0_gnn_h, L1_gnn_node_weight, L1_gnn_node_bias, L1_gnn_edge_weight, L1_gnn_edge_bias):
    import jax
    import jax.numpy as jnp

    def _L0_gnn_ref(x, adj, h):
        import jax, jax.numpy as jnp
        import numpy as np
        ALPHA = 0.1
        N, F = (8192, 128)
        return (1.0 - ALPHA) * (adj @ x) + ALPHA * h

    def _L1_gnn_ref(feats, node_adj, edge_adj, node_weight, node_bias, edge_weight, edge_bias):
        import jax, jax.numpy as jnp
        import numpy as np
        N = 6144
        F_IN = 128
        F_OUT = 128
        pos = (node_adj > 0).astype(feats.dtype)
        neg = (node_adj < 0).astype(feats.dtype)
        node_support = jnp.concatenate([pos @ feats, neg @ feats], axis=1)
        node_output = node_support @ node_weight + node_bias
        edge_support = edge_adj @ feats
        edge_output = edge_support @ edge_weight + edge_bias
        return jax.nn.relu(node_output) + edge_output
    x = _layernorm(x + _L0_gnn_ref(x, adj, L0_gnn_h), axis=-1)
    x = _layernorm(x + _L1_gnn_ref(x, adj, adj, L1_gnn_node_weight, L1_gnn_node_bias, L1_gnn_edge_weight, L1_gnn_edge_bias), axis=-1)
    return x

_drawn_inputs = setup_inputs


def setup_inputs(seed=0):
    import zlib

    import numpy as np

    out = dict(_drawn_inputs(seed))
    spreads = {}
    factors = {}
    for name, (base, spread) in spreads.items():
        noise = np.random.default_rng([zlib.crc32(name.encode()), seed]).standard_normal(out[name].shape)
        drawn = base * np.exp(spread * noise) if base else spread * noise
        out[name] = jnp.asarray(drawn.astype(out[name].dtype))
    for name, factor in factors.items():
        out[name] = (out[name] * factor).astype(out[name].dtype)
    return out
```

```python
import concourse.bass as bass
from concourse import mybir
from contextlib import ExitStack


def two_layer_graph_kernel(nc, x, adj, h, wn, bn, we, be, out):
    fp32 = mybir.dt.float32
    ALU = mybir.AluOpType
    ACT = mybir.ActivationFunctionType

    P = 128
    N, F = x.shape
    ALPHA, EPS = 0.1, 1e-5
    TILES = N // P
    CW = 512
    CB = CW // P
    SLOTS = 4
    TURNS = N // CW // SLOTS

    x_blocks = x.rearrange("(b p) f -> p b f", p=P)
    h_blocks = h.rearrange("(b p) f -> p b f", p=P)
    out_blocks = out.rearrange("(b p) f -> p b f", p=P)
    adj_tiles = adj.rearrange("(t p) (u s c) -> p t u s c", p=P, s=SLOTS, c=CW)

    ctx = ExitStack()
    with ctx:
        def sb(name, shape, dt=fp32):
            return ctx.enter_context(nc.sbuf_tensor(name, shape, dt))

        def pb(name, shape):
            return ctx.enter_context(nc.psum_tensor(name, shape, fp32))

        def sem(name):
            return ctx.enter_context(nc.semaphore(name))

        X = sb("X", [P, TILES, F])
        H = sb("H", [P, TILES, F])
        X1 = sb("X1", [P, TILES, F])
        chunk = [sb(f"chunk{s}", [P, CW]) for s in range(SLOTS)]
        adjT = [sb(f"adjT{i}", [P, CW]) for i in range(2)]
        posT = [sb(f"posT{i}", [P, CW]) for i in range(2)]
        negT = [sb(f"negT{i}", [P, CW]) for i in range(2)]
        ident = sb("ident", [P, P])
        zero = sb("zero", [P, P])
        ones = sb("ones", [1, P])
        Wn = sb("Wn", [P, 2, F])
        We = sb("We", [P, F])
        bn_row = sb("bn_row", [1, F])
        be_row = sb("be_row", [1, F])
        sums = sb("sums", [P, 3, F])
        sumsT = sb("sumsT", [P, 3, P])
        node = sb("node", [P, F])
        r = sb("r", [P, F])
        stats = sb("stats", [P, 6])
        mv = sb("mv", [P, 2])
        std = sb("std", [P, 1])
        rstd = sb("rstd", [P, 1])
        eps = sb("eps", [P, 1])

        tp = [pb(f"tp{i}", [P, CW]) for i in range(2)]
        acc = [pb(f"acc{i}", [P, 512]) for i in range(3)]
        tail = pb("tail", [P, 512])
        proj = pb("proj", [P, 512])

        const_ready = sem("const_ready")
        wait_carrier = sem("wait_carrier")
        weights_landed = sem("weights_landed")
        blocks_landed = sem("blocks_landed")
        out_landed = sem("out_landed")
        chunk_landed = {l: [sem(f"chunk_landed{l}_{s}") for s in range(SLOTS)] for l in (1, 2)}
        names = ["chunk_transposed", "adjT_ready", "adjT_used", "masks_ready",
                 "acc_ready", "acc_free", "sums_ready", "sumsT_made", "sumsT_ready", "proj_ready",
                 "node_ready", "var_ready", "std_ready", "tile_done", "step"]
        CHUNK0, ADJT0, USED0, FREE0 = SLOTS, 2, 2, 1
        S = {l: {n: sem(f"{n}_{l}") for n in names} for l in (1, 2)}

        block = ctx.enter_context(nc.Block())

        @block.sync
        def _(sp):
            sp.dma_start(X[:, :, :], x_blocks).then_inc(blocks_landed, 16)
            sp.dma_start(H[:, :, :], h_blocks).then_inc(blocks_landed, 16)
            sp.dma_start(Wn[:, :, :], wn.rearrange("(a p) f -> p a f", p=P)).then_inc(weights_landed, 16)
            sp.dma_start(We[:, :], we).then_inc(weights_landed, 16)
            sp.dma_start(bn_row[:, :], bn.rearrange("(a f) -> a f", a=1)).then_inc(weights_landed, 16)
            sp.dma_start(be_row[:, :], be.rearrange("(a f) -> a f", a=1)).then_inc(weights_landed, 16)
            for l in (1, 2):
                if l == 2:
                    sp.wait_ge(S[1]["chunk_transposed"], CHUNK0 + TILES * TURNS * SLOTS)
                sp.sem_inc(S[l]["chunk_transposed"], CHUNK0)
                with sp.Fori(0, TILES) as t:
                    with sp.Fori(0, TURNS) as u:
                        for s in range(SLOTS):
                            sp.wait_ge(S[l]["chunk_transposed"], (t * TURNS + u) * SLOTS + (s + 1))
                            sp.dma_start(chunk[s][:, :], adj_tiles[:, t, u, s, :]).then_inc(chunk_landed[l][s], 16)
                    if l == 2:
                        sp.wait_ge(S[2]["tile_done"], t + 1)
                        sp.dma_start(out_blocks[:, t, :], H[:, t, :]).then_inc(out_landed, 16)
            sp.wait_ge(out_landed, 16 * TILES)

        @block.gpsimd
        def _(pool):
            pool.memset(ident[:, :], 0.0).then_inc(const_ready, 1)
            pool.memset(ones[:, :], 1.0).then_inc(const_ready, 1)
            pool.memset(eps[:, :], EPS).then_inc(const_ready, 1)
            pool.memset(zero[:, :], 0.0).then_inc(const_ready, 1)
            pool.wait_ge(const_ready, 4)
            pool.affine_select(out=ident[:, :], in_=ident[:, :], compare_op=ALU.not_equal, fill=1.0,
                               base=0, pattern=[[-1, P]], channel_multiplier=1).then_inc(const_ready, 1)

        @block.tensor
        def _(pe):
            pe.wait_ge(const_ready, 5)
            pe.wait_ge(blocks_landed, 32)
            pe.wait_ge(weights_landed, 64)
            for l in (1, 2):
                q = S[l]
                rows = X if l == 1 else X1
                if l == 2:
                    pe.wait_ge(S[1]["tile_done"], TILES)

                def transposes(n, s, u_turn):
                    pe.wait_ge(chunk_landed[l][s], 16 * u_turn + 16)
                    pe.wait_ge(q["adjT_ready"], n + (ADJT0 - 1))
                    for b in range(CB):
                        last = nc.tensor.transpose(tp[s % 2][:, b * P:(b + 1) * P],
                                                   chunk[s][:, b * P:(b + 1) * P], ident[:, :])
                    last.then_inc(q["chunk_transposed"], 1)

                def products(n, s, u):
                    pe.wait_ge(q["adjT_ready"], n + (ADJT0 + 1))
                    if l == 2:
                        pe.wait_ge(q["masks_ready"], n + 1)
                    parts = [adjT] if l == 1 else [adjT, posT, negT]
                    for b in range(CB):
                        for a, part in enumerate(parts):
                            last = nc.tensor.matmul(acc[a][:, 0:F], part[s % 2][:, b * P:(b + 1) * P],
                                                    rows[:, u * (SLOTS * CB) + (s * CB + b), :],
                                                    start=False, stop=False, skip_group_check=True)
                    last.then_inc(q["adjT_used"], 1)

                with pe.Fori(0, TILES) as t:
                    pe.wait_ge(q["acc_free"], t + 1)
                    for a in range(1 if l == 1 else 3):
                        last = nc.tensor.matmul(acc[a][:, 0:F], zero[:, :], ident[:, :], start=True, stop=False,
                                         skip_group_check=True)
                    with pe.Fori(0, TURNS) as u:
                        turn = t * TURNS + u
                        n = turn * SLOTS
                        transposes(n, 0, turn)
                        for s in range(1, SLOTS):
                            transposes(n + s, s, turn)
                            products(n + (s - 1), s - 1, u)
                        products(n + (SLOTS - 1), SLOTS - 1, u)
                    for a in range(1 if l == 1 else 3):
                        last = nc.tensor.matmul(acc[a][:, 0:F], zero[:, :], ident[:, :], start=False, stop=True,
                                         skip_group_check=True)
                    last.then_inc(q["acc_ready"], 1)
                    if l == 2:
                        pe.wait_ge(q["sums_ready"], t + 1)
                        for a in range(3):
                            last = nc.tensor.transpose(tail[:, a * P:(a + 1) * P], sums[:, a, :], ident[:, :])
                        last.then_inc(q["sumsT_made"], 1)
                        pe.wait_ge(q["sumsT_ready"], t + 1)
                        nc.tensor.matmul(proj[:, 0:F], sumsT[:, 1, :], Wn[:, 0, :], start=True, stop=False)
                        nc.tensor.matmul(proj[:, 0:F], sumsT[:, 2, :], Wn[:, 1, :], start=False, stop=False)
                        nc.tensor.matmul(proj[:, 0:F], ones[:, :], bn_row[:, :], start=False, stop=True)
                        nc.tensor.matmul(proj[:, F:2 * F], sumsT[:, 0, :], We[:, :], start=True, stop=False)
                        nc.tensor.matmul(proj[:, F:2 * F], ones[:, :], be_row[:, :], start=False, stop=True)\
                            .then_inc(q["proj_ready"], 1)

        @block.scalar
        def _(act):
            act.wait_ge(const_ready, 5)
            for l in (1, 2):
                q = S[l]
                act.sem_inc(q["adjT_ready"], ADJT0)
                act.sem_inc(q["adjT_used"], USED0)
                with act.Fori(0, TILES) as t:
                    with act.Fori(0, TURNS) as u:
                        for s in range(SLOTS):
                            n = (t * TURNS + u) * SLOTS + s
                            act.wait_ge(q["chunk_transposed"], n + (CHUNK0 + 1))
                            act.wait_ge(q["adjT_used"], n + (USED0 - 1))
                            nc.scalar.activation(adjT[s % 2][:, :], tp[s % 2][:, :], ACT.Copy)\
                                .then_inc(q["adjT_ready"], 1)
                    if l == 2:
                        act.wait_ge(q["proj_ready"], t + 1)
                        nc.scalar.activation(node[:, :], proj[:, 0:F], ACT.Relu).then_inc(q["node_ready"], 1)
                    act.wait_ge(q["var_ready"], t + 1)
                    nc.scalar.activation(std[:, :], mv[:, 1:2], ACT.Sqrt, bias=eps[:, :]).then_inc(q["std_ready"], 1)

        @block.vector
        def _(dve):
            dve.wait_ge(blocks_landed, 32)
            for l in (1, 2):
                q = S[l]
                dve.sem_inc(q["acc_free"], FREE0)
                STEPS = 4
                with dve.Fori(0, TILES) as t:
                    done = [0]

                    def step(ins):
                        done[0] += 1
                        ins.then_inc(q["step"], 1)
                        dve.wait_ge(q["step"], t * STEPS + done[0])

                    if l == 2:
                        with dve.Fori(0, TURNS) as u:
                            for s in range(SLOTS):
                                n = (t * TURNS + u) * SLOTS + s
                                dve.wait_ge(q["adjT_ready"], n + (ADJT0 + 1))
                                dve.wait_ge(q["adjT_used"], n + (USED0 - 1))
                                nc.vector.tensor_scalar(posT[s % 2][:, :], adjT[s % 2][:, :], 0.0, None, ALU.is_gt)
                                nc.vector.tensor_scalar(negT[s % 2][:, :], adjT[s % 2][:, :], 0.0, None, ALU.is_lt)\
                                    .then_inc(q["masks_ready"], 1)
                    dve.wait_ge(q["acc_ready"], t + 1)
                    if l == 1:
                        step(nc.vector.scalar_tensor_tensor(r[:, :], acc[0][:, 0:F], 1.0 - ALPHA, X[:, t, :],
                                                            ALU.mult, ALU.add))
                        step(nc.vector.scalar_tensor_tensor(r[:, :], H[:, t, :], ALPHA, r[:, :],
                                                            ALU.mult, ALU.add))
                    else:
                        for a in range(3):
                            last = nc.vector.tensor_copy(sums[:, a, :], acc[a][:, 0:F])
                        last.then_inc(q["sums_ready"], 1)
                        dve.wait_ge(q["sumsT_made"], t + 1)
                        nc.vector.tensor_copy(sumsT[:, :, :], tail[:, 0:3 * P].rearrange("p (a i) -> p a i", a=3))\
                            .then_inc(q["sumsT_ready"], 1)
                        dve.wait_ge(q["node_ready"], t + 1)
                        step(nc.vector.tensor_tensor(r[:, :], node[:, :], proj[:, F:2 * F], ALU.add))
                        step(nc.vector.tensor_tensor(r[:, :], r[:, :], X1[:, t, :], ALU.add))
                        
                    step(nc.vector.bn_stats(stats[:, :], r[:, :]))
                    dve.sem_inc(wait_carrier, 1)
                    nc.vector.bn_aggr(mv[:, :], stats[:, :]).then_inc(q["var_ready"], 1)
                    dve.wait_ge(q["std_ready"], t + 1)
                    step(nc.vector.reciprocal(rstd[:, :], std[:, :]))
                    to = X1 if l == 1 else H
                    nc.vector.tensor_scalar(to[:, t, :], r[:, :], mv[:, 0:1], rstd[:, :], ALU.subtract, ALU.mult)\
                        .then_inc(q["tile_done"], 1)
                    dve.wait_ge(q["tile_done"], t + 1)
                    dve.sem_inc(q["acc_free"], 1)


_INS = ["x", "adj", "L0_gnn_h", "L1_gnn_node_weight", "L1_gnn_node_bias", "L1_gnn_edge_weight", "L1_gnn_edge_bias"]


def kernel(**inputs):
    import numpy as _np
    import concourse.bacc as _bacc
    from concourse import mybir as _mybir
    from concourse.bass_utils import run_bass_kernel_spmd as _run

    nc = _bacc.Bacc("TRN2", target_bir_lowering=False, num_devices=1)
    arrays, args = {}, []
    for name in _INS:
        a = _np.ascontiguousarray(inputs[name])
        arrays[f"in_{name}"] = a
        args.append(nc.dram_tensor(f"in_{name}", a.shape, _mybir.dt.from_np(a.dtype), kind="ExternalInput").ap())
    shape = inputs["x"].shape
    args.append(nc.dram_tensor("out_0", shape, _mybir.dt.float32, kind="ExternalOutput").ap())
    two_layer_graph_kernel(nc, *args)
    r = _run(nc, [arrays], core_ids=[0])
    return r.results[0]["out_0"]
```

```python
import concourse.bass as bass
from concourse import mybir
from contextlib import ExitStack


def two_layer_graph_kernel(nc, x, adj, h, wn, bn, we, be, out, x1_rows):
    fp32, bf16 = mybir.dt.float32, mybir.dt.bfloat16
    i32, u32 = mybir.dt.int32, mybir.dt.uint32
    ALU = mybir.AluOpType
    ACT = mybir.ActivationFunctionType
    AX = mybir.AxisListType

    P = 128
    N, F = x.shape
    ALPHA, EPS = 0.1, 1e-5
    TILES = N // P
    RING = 4
    QUARTERS = 4
    QW = N // QUARTERS
    NEG_PARTS = 4
    K = 16
    BLOCKS = 4
    EDGES = BLOCKS * P
    COLUMN, ROW, VALUE = range(3)
    CW = 512
    CB = CW // P
    SLOTS = 4
    TURNS = N // CW // SLOTS

    x_blocks = x.rearrange("(b p) f -> p b f", p=P)
    h_blocks = h.rearrange("(b p) f -> p b f", p=P)
    x1_blocks = x1_rows.rearrange("(b p) f -> p b f", p=P)
    out_blocks = out.rearrange("(b p) f -> p b f", p=P)
    adj_tiles = adj.rearrange("(t p) c -> p t c", p=P)
    adj_chunks = adj.rearrange("(t p) (u s c) -> p t u s c", p=P, s=SLOTS, c=CW)

    ctx = ExitStack()
    with ctx:
        def sb(name, shape, dt=fp32):
            return ctx.enter_context(nc.sbuf_tensor(name, shape, dt))

        def sem(name):
            return ctx.enter_context(nc.semaphore(name))

        ident = sb("ident", [P, P])
        ones = sb("ones", [P, P])
        before = sb("before", [P, P])
        edge_at = sb("edge_at", [P, K + EDGES])
        row_no = sb("row_no", [P, P])
        my_row = sb("my_row", [P, K])
        Wn = sb("Wn", [P, 2, F])
        We = sb("We", [P, F])
        bn_row = sb("bn_row", [1, F])
        be_row = sb("be_row", [1, F])
        eps = sb("eps", [P, 1])

        A = [sb(f"adj{s}", [P, N]) for s in range(RING)]
        negatives = sb("negatives", [P, N // NEG_PARTS], bf16)
        cand = [sb(f"cand{i}", [P, QUARTERS, 8]) for i in range(2)]
        rest = [sb(f"rest{i}", [P, QUARTERS * 8]) for i in range(2)]
        top = [sb(f"top{i}", [P, K]) for i in range(2)]
        col = [sb(f"col{i}", [P, K], u32) for i in range(2)]
        col_f = [sb(f"col_f{i}", [P, K]) for i in range(2)]
        held = [sb(f"held{i}", [P, K]) for i in range(2)]
        deg = [sb(f"deg{i}", [P, 1]) for i in range(2)]
        more = [sb(f"more{i}", [1, 1], i32) for i in range(2)]
        entry = [sb(f"entry{i}", [P, K, 3]) for i in range(2)]
        place = [sb(f"place{i}", [P, K + EDGES]) for i in range(2)]
        rec = [sb(f"rec{i}", [P, BLOCKS, 3]) for i in range(2)]
        edge_col4 = [sb(f"edge_col_layer2_{s}", [P, BLOCKS], u32) for s in range(RING)]
        edge_col = [sb(f"edge_col{i}", [P, BLOCKS], u32) for i in range(2)]
        records = sb("records", [P, TILES + 1, BLOCKS, 3])
        tops = sb("tops", [P, TILES, K])
        eighths = sb("eighths", [P, TILES, QUARTERS])
        ends = sb("ends", [P, TILES, 1])
        neg_sums = sb("neg_sums", [P, TILES, NEG_PARTS])
        G = [sb(f"gathered{s}", [P, BLOCKS, F]) for s in range(RING)]
        pick = [sb(f"pick{i}", [P, BLOCKS, 2, P]) for i in range(2)]
        X1 = sb("X1", [P, TILES, F])
        xh = [sb(f"xh{s}", [P, F]) for s in range(RING)]
        ht = [sb(f"ht{s}", [P, F]) for s in range(RING)]
        r = [sb(f"r{i}", [P, F]) for i in range(2)]
        stats = [sb(f"stats{i}", [P, 6]) for i in range(2)]
        mv = [sb(f"mv{i}", [P, 2]) for i in range(2)]
        std = [sb(f"std{i}", [P, 1]) for i in range(2)]
        rstd = [sb(f"rstd{i}", [P, 1]) for i in range(2)]
        sumsT2 = [A[i][:, 0:2 * P].rearrange("p (a i) -> p a i", a=2) for i in range(2)]
        bad = sb("bad", [P, 6])
        bad_any = sb("bad_any", [P, 1])
        tie = sb("tie", [P, TILES])
        verdict = sb("verdict", [1, 1], i32)

        bank = [ctx.enter_context(nc.psum_tensor(f"bank{i}", [P, 512], fp32)) for i in range(8)]
        counts = bank[0:2]
        packed = bank[2:4]
        acc1 = bank[4:6]
        sums2 = bank[2:4]
        proj2 = bank[4:6]
        judged = bank[6]

        wait_carrier = sem("wait_carrier")

        def hold(eng, s, value):
            eng.wait_ge(s, value)
            eng.sem_inc(wait_carrier, 1)

        const_ready = sem("const_ready")
        weights_landed = sem("weights_landed")
        adj_landed = [sem(f"adj_landed{s}") for s in range(RING)]
        rows_landed = [sem(f"rows_landed{s}") for s in range(RING)]
        gathered = [sem(f"gathered{s}_1") for s in range(RING)]
        gathered2 = [sem(f"gathered{s}_2") for s in range(RING)]
        out_landed = sem("out_landed")
        x1_landed = sem("x1_landed")
        top_ready = sem("top_ready")
        counts_ready = sem("counts_ready")
        scanned = sem("scanned")
        neg_scanned = sem("neg_scanned")
        place_ready = sem("place_ready")
        col_f_ready = sem("col_f_ready")
        entry_ready = sem("entry_ready")
        packed_ready = sem("packed_ready")
        rec_ready = sem("rec_ready")
        edge_col_ready = sem("edge_col_ready")
        xh_ready = sem("xh_ready")
        pick_ready = sem("pick_ready")
        acc_ready = sem("acc_ready")
        var_ready = sem("var_ready")
        std_ready = sem("std_ready")
        x1_ready = sem("x1_ready")
        scan_step = sem("scan_step")
        more_step = sem("more_step")
        norm_step = sem("norm_step")
        scale_step = sem("scale_step")
        pool_step = sem("pool_step")
        edge_col2_ready = sem("edge_col2_ready")
        pick2_ready = sem("pick2_ready")
        sums2_ready = sem("sums2_ready")
        sumsT2_ready = sem("sumsT2_ready")
        proj2_ready = sem("proj2_ready")
        var2_ready = sem("var2_ready")
        std2_ready = sem("std2_ready")
        result_ready = sem("result_ready")
        norm2_step = sem("norm2_step")
        verdict_step = sem("verdict_step")
        bad_ready = sem("bad_ready")
        judged_ready = sem("judged_ready")
        verdict_ready = sem("verdict_ready")
        RING0, PAIR0 = RING, 2

        gX, gH, gX1 = [A[a][:, :].rearrange("p (b f) -> p b f", f=F) for a in range(3)]
        chunk = [A[3][:, a * CW:(a + 1) * CW] for a in range(SLOTS)]
        adjT, posT, negT = [[A[3][:, a * CW:(a + 1) * CW] for a in (SLOTS + m, SLOTS + m + 1)] for m in (0, 2, 4)]
        sums, sumsT = G[0][:, 0:3, :], G[1][:, 0:3, :]
        g_node, g_r, g_stats, g_mv, g_std, g_rstd = ht[0], r[0], stats[0], mv[0], std[0], rstd[0]
        tp, acc, tail, proj = bank[0:2], bank[2:5], bank[5], bank[6]
        zero = A[3][:, 12 * CW:12 * CW + P]
        zero_ready = sem("general_zero_ready")
        g_blocks_landed = sem("general_blocks_landed")
        g_out_landed = sem("general_out_landed")
        chunk_landed = {l: [sem(f"chunk_landed{l}_{s}") for s in range(SLOTS)] for l in (1, 2)}
        names = ["chunk_transposed", "adjT_ready", "adjT_used", "masks_ready",
                 "acc_ready", "acc_free", "sums_ready", "sumsT_made", "sumsT_ready", "proj_ready",
                 "node_ready", "var_ready", "std_ready", "tile_done", "step"]
        S = {l: {n: sem(f"general_{n}_{l}") for n in names} for l in (1, 2)}
        CHUNK0, ADJT0, USED0, FREE0 = SLOTS, 2, 2, 1

        block = ctx.enter_context(nc.Block())

        @block.sync
        def _(sp):
            sp.dma_start(Wn[:, :, :], wn.rearrange("(a p) f -> p a f", p=P)).then_inc(weights_landed, 16)
            sp.dma_start(We[:, :], we).then_inc(weights_landed, 16)
            sp.dma_start(bn_row[:, :], bn.rearrange("(a f) -> a f", a=1)).then_inc(weights_landed, 16)
            sp.dma_start(be_row[:, :], be.rearrange("(a f) -> a f", a=1)).then_inc(weights_landed, 16)
            for s in (scanned, var_ready):
                sp.sem_inc(s, RING0)
            sp.sem_inc(neg_scanned, RING0 * NEG_PARTS)
            with sp.Fori(0, TILES // RING) as turn:
                for s in range(RING):
                    t = turn * RING + s
                    hold(sp, scanned, t + 1)
                    hold(sp, neg_scanned, (t + 1) * NEG_PARTS)
                    sp.dma_start(A[s][:, :], adj_tiles[:, t, :]).then_inc(adj_landed[s], 16)
                    hold(sp, var_ready, t + 1)
                    sp.dma_start(xh[s][:, :], x_blocks[:, t, :]).then_inc(rows_landed[s], 16)
                    sp.dma_start(ht[s][:, :], h_blocks[:, t, :]).then_inc(rows_landed[s], 16)
            half = TILES - 8
            sp.wait_ge(x1_ready, half)
            sp.dma_start(x1_blocks[:, 0:half, :], X1[:, 0:half, :]).then_inc(x1_landed, 16)
            sp.wait_ge(x1_ready, TILES)
            sp.dma_start(x1_blocks[:, half:TILES, :], X1[:, half:TILES, :]).then_inc(x1_landed, 16)
            with sp.Fori(0, TILES) as t:
                hold(sp, result_ready, t + 1)
                sp.dma_start(out_blocks[:, t, :], X1[:, t, :]).then_inc(out_landed, 16)
            sp.wait_ge(out_landed, 16 * TILES)

            sp.wait_ge(verdict_ready, 1)
            general = sp.value_load(verdict[0:1, 0:1], min_val=0, max_val=1)
            with sp.If(general > 0):
                sp.dma_start(gX, x_blocks).then_inc(g_blocks_landed, 16)
                sp.dma_start(gH, h_blocks).then_inc(g_blocks_landed, 16)
                for l in (1, 2):
                    if l == 2:
                        sp.wait_ge(S[1]["chunk_transposed"], CHUNK0 + TILES * TURNS * SLOTS)
                    sp.sem_inc(S[l]["chunk_transposed"], CHUNK0)
                    with sp.Fori(0, TILES) as t:
                        with sp.Fori(0, TURNS) as u:
                            for s in range(SLOTS):
                                sp.wait_ge(S[l]["chunk_transposed"], (t * TURNS + u) * SLOTS + (s + 1))
                                sp.dma_start(chunk[s], adj_chunks[:, t, u, s, :]).then_inc(chunk_landed[l][s], 16)
                        if l == 2:
                            sp.wait_ge(S[2]["tile_done"], t + 1)
                            sp.dma_start(out_blocks[:, t, :], gH[:, t, :]).then_inc(g_out_landed, 16)
                sp.wait_ge(g_out_landed, 16 * TILES)

        @block.gpsimd
        def _(pool):
            pool.memset(ident[:, :], 0.0).then_inc(const_ready, 1)
            pool.memset(ones[:, :], 1.0).then_inc(const_ready, 1)
            pool.memset(before[:, :], 1.0).then_inc(const_ready, 1)
            pool.memset(eps[:, :], EPS).then_inc(const_ready, 1)
            pool.memset(records[:, TILES, :, :], 0.0).then_inc(const_ready, 1)
            for i in range(2):
                pool.memset(col[i][:, :], 0).then_inc(const_ready, 1)
            pool.iota(edge_at[:, :], [[1, K + EDGES]], base=-K, channel_multiplier=0,
                      allow_small_or_imprecise_dtypes=True).then_inc(const_ready, 1)
            pool.iota(row_no[:, :], [[1, P]], base=1, channel_multiplier=0,
                      allow_small_or_imprecise_dtypes=True).then_inc(const_ready, 1)
            pool.iota(my_row[:, :], [[0, K]], base=1, channel_multiplier=1,
                      allow_small_or_imprecise_dtypes=True).then_inc(const_ready, 1)
            pool.wait_ge(const_ready, 10)
            pool.affine_select(out=ident[:, :], in_=ident[:, :], compare_op=ALU.not_equal, fill=1.0,
                               base=0, pattern=[[-1, P]], channel_multiplier=1).then_inc(const_ready, 1)
            pool.affine_select(out=before[:, :], in_=before[:, :], compare_op=ALU.is_gt, fill=0.0,
                               base=0, pattern=[[1, P]], channel_multiplier=-1).then_inc(const_ready, 1)
            pool.sem_inc(packed_ready, PAIR0)
            pool.sem_inc(acc_ready, RING0)
            with pool.Fori(0, TILES // RING) as turn:
                for s in range(RING):
                    t, i = turn * RING + s, s % 2
                    hold(pool, rows_landed[s], turn * 32 + 32)
                    nc.gpsimd.tensor_scalar(ht[s][:, :], ht[s][:, :], ALPHA, None, ALU.mult).then_inc(pool_step, 1)
                    pool.wait_ge(pool_step, t * 1 + 1)
                    nc.gpsimd.tensor_tensor(xh[s][:, :], xh[s][:, :], ht[s][:, :], ALU.add).then_inc(xh_ready, 1)
                    pool.wait_ge(scanned, t + (RING0 + 1))
                    hold(pool, packed_ready, t + (PAIR0 - 1))
                    nc.gpsimd.tensor_copy(col_f[i][:, :], col[i][:, :]).then_inc(col_f_ready, 1)
                    pool.wait_ge(col_f_ready, t + 1)
                    nc.gpsimd.tensor_tensor(entry[i][:, :, COLUMN], col_f[i][:, :], held[i][:, :], ALU.mult)
                    nc.gpsimd.tensor_tensor(entry[i][:, :, ROW], my_row[:, :], held[i][:, :], ALU.mult)
                    nc.gpsimd.tensor_copy(entry[i][:, :, VALUE], top[i][:, :])
                    nc.gpsimd.tensor_copy(tops[:, t, :], top[i][:, :])
                    nc.gpsimd.tensor_copy(eighths[:, t, :], cand[i][:, :, 7]).then_inc(entry_ready, 1)
                    hold(pool, rec_ready, t + 1)
                    nc.gpsimd.tensor_copy(edge_col[i][:, :], rec[i][:, :, COLUMN]).then_inc(edge_col_ready, 1)
                    hold(pool, edge_col_ready, t + 1)
                    hold(pool, acc_ready, t + 1)
                    for b in range(BLOCKS):
                        nc.gpsimd.indirect_dma_start(
                            out=G[s][:, b, :], out_offset=None, in_=x,
                            in_offset=bass.IndirectOffsetOnAxis(ap=edge_col[i][:, b:b + 1], axis=0),
                            bounds_check=N - 1, oob_is_err=False).then_inc(gathered[s], 16)
                    hold(pool, acc_ready, t + (RING0 - 1))
                    for b in range(BLOCKS):
                        nc.gpsimd.tensor_scalar(pick[i][:, b, 1, :], row_no[:, :], rec[i][:, b, ROW:ROW + 1],
                                                rec[i][:, b, VALUE:VALUE + 1], ALU.is_equal, ALU.mult)
                    nc.gpsimd.tensor_copy(records[:, t, :, :], rec[i][:, :, :]).then_inc(pick_ready, 1)
            pool.wait_ge(acc_ready, RING0 + TILES)
            pool.wait_ge(pick_ready, TILES)
            pool.wait_ge(x1_landed, 32)
            pool.sem_inc(sums2_ready, RING0)
            with pool.Fori(0, TILES // RING) as turn:
                for s in range(RING):
                    t, i = turn * RING + s, s % 2
                    hold(pool, sums2_ready, t + 1)
                    nc.gpsimd.tensor_copy(edge_col4[s][:, :], records[:, t, :, COLUMN]).then_inc(edge_col2_ready, 1)
                    hold(pool, edge_col2_ready, t + 1)
                    for b in range(BLOCKS):
                        nc.gpsimd.indirect_dma_start(
                            out=G[s][:, b, :], out_offset=None, in_=x1_rows,
                            in_offset=bass.IndirectOffsetOnAxis(ap=edge_col4[s][:, b:b + 1], axis=0),
                            bounds_check=N - 1, oob_is_err=False).then_inc(gathered2[s], 16)

        @block.tensor
        def _(pe):
            pe.wait_ge(const_ready, 12)
            pe.wait_ge(weights_landed, 64)
            with pe.Fori(0, TILES // RING) as turn:
                for s in range(RING):
                    t, i = turn * RING + s, s % 2
                    pe.wait_ge(top_ready, t + 1)
                    nc.tensor.matmul(counts[i][:, 0:1], before[:, :], deg[i][:, :], start=True, stop=True)
                    nc.tensor.matmul(counts[i][:, 1:2], ones[:, :], top[i][:, 8:9], start=True, stop=True)\
                        .then_inc(counts_ready, 1)
                    pe.wait_ge(place_ready, t + 1)
                    pe.wait_ge(entry_ready, t + 1)
                    for b in range(BLOCKS):
                        for k in range(K):
                            at = K - k + b * P
                            last = nc.tensor.matmul(packed[i][:, 3 * b:3 * b + 3], place[i][:, at:at + P],
                                                    entry[i][:, k, :], start=(k == 0), stop=(k == K - 1))
                    last.then_inc(packed_ready, 1)
                    pe.wait_ge(gathered[s], turn * (16 * BLOCKS) + 16 * BLOCKS)
                    pe.wait_ge(pick_ready, t + 1)
                    pe.wait_ge(var_ready, t + (RING0 - 1))
                    for b in range(BLOCKS):
                        last = nc.tensor.matmul(acc1[i][:, 0:F], pick[i][:, b, 1, :], G[s][:, b, :],
                                                start=(b == 0), stop=(b == BLOCKS - 1))
                    last.then_inc(acc_ready, 1)
            pe.sem_inc(sumsT2_ready, PAIR0)
            pe.sem_inc(var2_ready, PAIR0)
            with pe.Fori(0, TILES // RING) as turn:
                for s in range(RING):
                    t, i = turn * RING + s, s % 2
                    pe.wait_ge(gathered2[s], turn * (16 * BLOCKS) + 16 * BLOCKS)
                    pe.wait_ge(pick2_ready, t + 1)
                    pe.wait_ge(sumsT2_ready, t + (PAIR0 - 1))
                    for b in range(BLOCKS):
                        last = nc.tensor.matmul(sums2[i][:, 0:2 * P], G[s][:, b, :], pick[i][:, b, :, :],
                                                start=(b == 0), stop=(b == BLOCKS - 1))
                    last.then_inc(sums2_ready, 1)
                    pe.wait_ge(sumsT2_ready, t + (PAIR0 + 1))
                    pe.wait_ge(var2_ready, t + (PAIR0 - 1))
                    nc.tensor.matmul(proj2[i][:, 0:F], sumsT2[i][:, 0, :], Wn[:, 0, :], start=True, stop=False)
                    nc.tensor.matmul(proj2[i][:, 0:F], ones[0:1, :], bn_row[:, :], start=False, stop=True)
                    nc.tensor.matmul(proj2[i][:, F:2 * F], sumsT2[i][:, 1, :], We[:, :], start=True, stop=False)
                    nc.tensor.matmul(proj2[i][:, F:2 * F], ident[:, :], X1[:, t, :], start=False, stop=False)
                    nc.tensor.matmul(proj2[i][:, F:2 * F], ones[0:1, :], be_row[:, :], start=False, stop=True)\
                        .then_inc(proj2_ready, 1)
            pe.wait_ge(bad_ready, 1)
            nc.tensor.matmul(judged[:, 0:1], ones[:, :], bad_any[:, :], start=True, stop=True).then_inc(judged_ready, 1)

            pe.wait_ge(verdict_ready, 1)
            general = pe.value_load(verdict[0:1, 0:1], min_val=0, max_val=1)
            with pe.If(general > 0):
                pe.wait_ge(g_blocks_landed, 32)
                pe.wait_ge(zero_ready, 1)
                for l in (1, 2):
                    q = S[l]
                    rows = gX if l == 1 else gX1
                    if l == 2:
                        pe.wait_ge(S[1]["tile_done"], TILES)

                    def transposes(n, s, u_turn):
                        pe.wait_ge(chunk_landed[l][s], 16 * u_turn + 16)
                        pe.wait_ge(q["adjT_ready"], n + (ADJT0 - 1))
                        for b in range(CB):
                            last = nc.tensor.transpose(tp[s % 2][:, b * P:(b + 1) * P],
                                                       chunk[s][:, b * P:(b + 1) * P], ident[:, :])
                        last.then_inc(q["chunk_transposed"], 1)

                    def products(n, s, u):
                        pe.wait_ge(q["adjT_ready"], n + (ADJT0 + 1))
                        if l == 2:
                            pe.wait_ge(q["masks_ready"], n + 1)
                        parts = [adjT] if l == 1 else [adjT, posT, negT]
                        for b in range(CB):
                            for a, part in enumerate(parts):
                                last = nc.tensor.matmul(acc[a][:, 0:F], part[s % 2][:, b * P:(b + 1) * P],
                                                        rows[:, u * (SLOTS * CB) + (s * CB + b), :],
                                                        start=False, stop=False, skip_group_check=True)
                        last.then_inc(q["adjT_used"], 1)

                    with pe.Fori(0, TILES) as t:
                        pe.wait_ge(q["acc_free"], t + 1)
                        for a in range(1 if l == 1 else 3):
                            last = nc.tensor.matmul(acc[a][:, 0:F], zero, ident[:, :], start=True, stop=False,
                                             skip_group_check=True)
                        with pe.Fori(0, TURNS) as u:
                            turn = t * TURNS + u
                            n = turn * SLOTS
                            transposes(n, 0, turn)
                            for s in range(1, SLOTS):
                                transposes(n + s, s, turn)
                                products(n + (s - 1), s - 1, u)
                            products(n + (SLOTS - 1), SLOTS - 1, u)
                        for a in range(1 if l == 1 else 3):
                            last = nc.tensor.matmul(acc[a][:, 0:F], zero, ident[:, :], start=False, stop=True,
                                             skip_group_check=True)
                        last.then_inc(q["acc_ready"], 1)
                        if l == 2:
                            pe.wait_ge(q["sums_ready"], t + 1)
                            for a in range(3):
                                last = nc.tensor.transpose(tail[:, a * P:(a + 1) * P], sums[:, a, :], ident[:, :])
                            last.then_inc(q["sumsT_made"], 1)
                            pe.wait_ge(q["sumsT_ready"], t + 1)
                            nc.tensor.matmul(proj[:, 0:F], sumsT[:, 1, :], Wn[:, 0, :], start=True, stop=False)
                            nc.tensor.matmul(proj[:, 0:F], sumsT[:, 2, :], Wn[:, 1, :], start=False, stop=False)
                            nc.tensor.matmul(proj[:, 0:F], ones[0:1, :], bn_row[:, :], start=False, stop=True)
                            nc.tensor.matmul(proj[:, F:2 * F], sumsT[:, 0, :], We[:, :], start=True, stop=False)
                            nc.tensor.matmul(proj[:, F:2 * F], ones[0:1, :], be_row[:, :], start=False, stop=True)\
                                .then_inc(q["proj_ready"], 1)

        @block.scalar
        def _(act):
            act.wait_ge(const_ready, 12)

            def below_zero(t, s, own_turn):
                act.wait_ge(adj_landed[s], own_turn * 16 + 16)
                for a in range(NEG_PARTS):
                    act.wait_ge(neg_scanned, (t + RING) * NEG_PARTS + a)
                    nc.scalar.activation(negatives[:, :], A[s][:, a * QW:(a + 1) * QW], ACT.Relu,
                                         scale=-1.0, accum_out=neg_sums[:, t, a:a + 1]).then_inc(neg_scanned, 1)

            def tile_records(t, i):
                act.wait_ge(packed_ready, t + (PAIR0 + 1))
                act.wait_ge(acc_ready, t + (RING0 - 1))
                nc.scalar.activation(rec[i][:, :, :], packed[i][:, 0:3 * BLOCKS].rearrange("p (b c) -> p b c", c=3),
                                     ACT.Copy).then_inc(rec_ready, 1)

            def deviation(t, i):
                act.wait_ge(var_ready, t + (RING0 + 1))
                nc.scalar.activation(std[i][:, :], mv[i][:, 1:2], ACT.Sqrt, bias=eps[:, :]).then_inc(std_ready, 1)

            below_zero(0, 0, 0)
            with act.Fori(0, TILES // RING - 1) as turn:
                for s in range(RING):
                    tile_records(turn * RING + s, s % 2)
                    below_zero(turn * RING + (s + 1), (s + 1) % RING, turn if s < RING - 1 else turn + 1)
                    deviation(turn * RING + s, s % 2)
            for s in range(RING):
                t = TILES - RING + s
                tile_records(t, s % 2)
                if t + 1 < TILES:
                    below_zero(t + 1, s + 1, TILES // RING - 1)
                deviation(t, s % 2)
            with act.Fori(0, TILES // RING) as turn:
                for s in range(RING):
                    t, i = turn * RING + s, s % 2
                    act.wait_ge(sums2_ready, t + (RING0 + 1))
                    nc.scalar.activation(sumsT2[i], sums2[i][:, 0:2 * P].rearrange("p (a i) -> p a i", a=2),
                                         ACT.Copy).then_inc(sumsT2_ready, 1)
                    act.wait_ge(var2_ready, t + (PAIR0 + 1))
                    nc.scalar.activation(std[i][:, :], mv[i][:, 1:2], ACT.Sqrt, bias=eps[:, :]).then_inc(std2_ready, 1)

            act.wait_ge(verdict_ready, 1)
            general = act.value_load(verdict[0:1, 0:1], min_val=0, max_val=1)
            with act.If(general > 0):
                for l in (1, 2):
                    q = S[l]
                    act.sem_inc(q["adjT_ready"], ADJT0)
                    act.sem_inc(q["adjT_used"], USED0)
                    with act.Fori(0, TILES) as t:
                        with act.Fori(0, TURNS) as u:
                            for s in range(SLOTS):
                                n = (t * TURNS + u) * SLOTS + s
                                act.wait_ge(q["chunk_transposed"], n + (CHUNK0 + 1))
                                act.wait_ge(q["adjT_used"], n + (USED0 - 1))
                                nc.scalar.activation(adjT[s % 2], tp[s % 2][:, :], ACT.Copy)\
                                    .then_inc(q["adjT_ready"], 1)
                        if l == 2:
                            act.wait_ge(q["proj_ready"], t + 1)
                            nc.scalar.activation(g_node[:, :], proj[:, 0:F], ACT.Relu).then_inc(q["node_ready"], 1)
                        act.wait_ge(q["var_ready"], t + 1)
                        nc.scalar.activation(g_std[:, :], g_mv[:, 1:2], ACT.Sqrt, bias=eps[:, :]).then_inc(q["std_ready"], 1)

        @block.vector
        def _(dve):
            dve.wait_ge(const_ready, 12)

            def largest(t, s, turn):
                i = s % 2
                hold(dve, adj_landed[s], turn * 16 + 16)
                if not (isinstance(t, int) and t < 2):
                    hold(dve, entry_ready, t - 1)
                for c in range(QUARTERS):
                    last = nc.vector.max(cand[i][:, c, :], A[s][:, c * QW:(c + 1) * QW])
                last.then_inc(scan_step, 1)
                hold(dve, scan_step, t * 3 + 1)
                nc.vector.max(top[i][:, 0:8], cand[i][:, :, :]).then_inc(scan_step, 1)
                hold(dve, scan_step, t * 3 + 2)
                nc.vector.match_replace(rest[i][:, :], top[i][:, 0:8], cand[i][:, :, :].rearrange("p a b -> p (a b)"), 0.0)\
                    .then_inc(scan_step, 1)
                hold(dve, scan_step, t * 3 + 3)
                nc.vector.max(top[i][:, 8:16], rest[i][:, :]).then_inc(more_step, 1)
                dve.wait_ge(more_step, t * 4 + 1)
                nc.vector.tensor_scalar(held[i][:, :], top[i][:, :], 0.0, 0.0, ALU.is_gt, ALU.add,
                                        accum_out=deg[i][:, :]).then_inc(top_ready, 1)

            def columns(t, s, turn):
                i = s % 2
                nc.vector.max_index(col[i][:, 0:8], top[i][:, 0:8], A[s][:, :]).then_inc(more_step, 1)
                dve.wait_ge(counts_ready, t + 1)
                nc.vector.tensor_scalar(more[i][:, :], counts[i][0:1, 1:2], 0.0, None, ALU.is_gt).then_inc(more_step, 1)
                dve.wait_ge(packed_ready, t + (PAIR0 - 1))
                nc.vector.tensor_scalar(place[i][:, :], edge_at[:, :], counts[i][:, 0:1], None, ALU.is_equal)\
                    .then_inc(place_ready, 1)
                nc.vector.tensor_tensor(ends[:, t, :], counts[i][:, 0:1], deg[i][:, :], ALU.add).then_inc(more_step, 1)
                hold(dve, more_step, t * 4 + 4)
                some_more = dve.value_load(more[i][0:1, 0:1], min_val=0, max_val=1)
                with dve.If(some_more > 0):
                    nc.vector.max_index(col[i][:, 8:16], top[i][:, 8:16], A[s][:, :]).then_inc(scanned, 1)
                with dve.Else():
                    dve.sem_inc(scanned, 1)

            def moments(t, s):
                i = s % 2
                dve.wait_ge(xh_ready, t + 1)
                dve.wait_ge(acc_ready, t + (RING0 + 1))
                nc.vector.scalar_tensor_tensor(r[i][:, :], acc1[i][:, 0:F], 1.0 - ALPHA, xh[s][:, :],
                                               ALU.mult, ALU.add).then_inc(norm_step, 1)
                dve.wait_ge(norm_step, t * 2 + 1)
                nc.vector.bn_stats(stats[i][:, :], r[i][:, :]).then_inc(norm_step, 1)
                hold(dve, norm_step, t * 2 + 2)
                nc.vector.bn_aggr(mv[i][:, :], stats[i][:, :]).then_inc(var_ready, 1)

            def scaled(t, s):
                i = s % 2
                dve.wait_ge(std_ready, t + 1)
                nc.vector.reciprocal(rstd[i][:, :], std[i][:, :]).then_inc(scale_step, 1)
                dve.wait_ge(scale_step, t + 1)
                nc.vector.tensor_scalar(X1[:, t, :], r[i][:, :], mv[i][:, 0:1], rstd[i][:, :],
                                        ALU.subtract, ALU.mult).then_inc(x1_ready, 1)

            largest(0, 0, 0)
            columns(0, 0, 0)
            largest(1, 1, 0)
            columns(1, 1, 0)
            moments(0, 0)
            BODIES = (TILES - 4) // RING
            with dve.Fori(0, BODIES) as turn:
                for j in range(RING):
                    t, s = turn * RING + (j + 2), (j + 2) % RING
                    own_turn = turn if j < 2 else turn + 1
                    largest(t, s, own_turn)
                    scaled(turn * RING + j, j)
                    columns(t, s, own_turn)
                    moments(turn * RING + (j + 1), (j + 1) % RING)
            for t in (TILES - 2, TILES - 1):
                s = t % RING
                largest(t, s, t // RING)
                scaled(t - 2, (t - 2) % RING)
                columns(t, s, t // RING)
                moments(t - 1, (t - 1) % RING)
            scaled(TILES - 2, RING - 2)
            moments(TILES - 1, RING - 1)
            scaled(TILES - 1, RING - 1)

            dve.wait_ge(entry_ready, TILES)
            dve.wait_ge(neg_scanned, (RING0 + TILES) * NEG_PARTS)
            nc.vector.tensor_reduce(bad[:, 0:1], tops[:, :, K - 1], AX.X, ALU.max)
            nc.vector.tensor_reduce(bad[:, 1:2], eighths[:, :, :], AX.XY, ALU.max)
            nc.vector.tensor_scalar(ends[:, :, 0], ends[:, :, 0], float(EDGES), None, ALU.is_gt).then_inc(verdict_step, 1)
            nc.vector.tensor_reduce(bad[:, 3:4], neg_sums[:, :, :], AX.XY, ALU.add)
            nc.vector.tensor_tensor(tie[:, :], tops[:, :, 7], tops[:, :, 8], ALU.is_equal).then_inc(verdict_step, 1)
            dve.wait_ge(verdict_step, 2)
            nc.vector.tensor_reduce(bad[:, 2:3], ends[:, :, 0], AX.X, ALU.max)
            nc.vector.tensor_tensor(tie[:, :], tie[:, :], tops[:, :, 8], ALU.mult).then_inc(verdict_step, 1)
            dve.wait_ge(verdict_step, 3)
            nc.vector.tensor_reduce(bad[:, 4:5], tie[:, :], AX.X, ALU.max).then_inc(verdict_step, 1)
            dve.wait_ge(verdict_step, 4)
            nc.vector.tensor_scalar(bad[:, 0:5], bad[:, 0:5], 0.0, None, ALU.not_equal).then_inc(verdict_step, 1)
            dve.wait_ge(verdict_step, 5)
            nc.vector.tensor_reduce(bad_any[:, :], bad[:, 0:5], AX.X, ALU.add).then_inc(bad_ready, 1)

            dve.wait_ge(pick_ready, TILES)

            def picks(t, s):
                i = s % 2
                dve.wait_ge(sums2_ready, t + (RING0 - 1))
                for b in range(BLOCKS):
                    nc.vector.tensor_scalar(pick[i][:, b, 0, :], row_no[:, :], records[:, t, b, ROW:ROW + 1], None,
                                            ALU.is_equal)
                    last = nc.vector.tensor_scalar(pick[i][:, b, 1, :], row_no[:, :], records[:, t, b, ROW:ROW + 1],
                                                   records[:, t, b, VALUE:VALUE + 1], ALU.is_equal, ALU.mult)
                last.then_inc(pick2_ready, 1)

            dve.wait_ge(acc_ready, RING0 + TILES)
            picks(0, 0)
            with dve.Fori(0, TILES // RING) as turn:
                for s in range(RING):
                    t, i = turn * RING + s, s % 2
                    picks(turn * RING + (s + 1), s + 1)
                    dve.wait_ge(proj2_ready, t + 1)
                    nc.vector.tensor_scalar(r[i][:, :], proj2[i][:, 0:F], 0.0, None, ALU.max).then_inc(norm2_step, 1)
                    dve.wait_ge(norm2_step, t * 4 + 1)
                    nc.vector.tensor_tensor(r[i][:, :], r[i][:, :], proj2[i][:, F:2 * F], ALU.add).then_inc(norm2_step, 1)
                    dve.wait_ge(norm2_step, t * 4 + 2)
                    nc.vector.bn_stats(stats[i][:, :], r[i][:, :]).then_inc(norm2_step, 1)
                    hold(dve, norm2_step, t * 4 + 3)
                    nc.vector.bn_aggr(mv[i][:, :], stats[i][:, :]).then_inc(var2_ready, 1)
                    dve.wait_ge(std2_ready, t + 1)
                    nc.vector.reciprocal(rstd[i][:, :], std[i][:, :]).then_inc(norm2_step, 1)
                    dve.wait_ge(norm2_step, t * 4 + 4)
                    nc.vector.tensor_scalar(X1[:, t, :], r[i][:, :], mv[i][:, 0:1], rstd[i][:, :],
                                            ALU.subtract, ALU.mult).then_inc(result_ready, 1)
            dve.wait_ge(judged_ready, 1)
            nc.vector.tensor_scalar(verdict[:, :], judged[0:1, 0:1], 0.0, None, ALU.is_gt).then_inc(verdict_ready, 1)

            dve.wait_ge(verdict_ready, 1)
            general = dve.value_load(verdict[0:1, 0:1], min_val=0, max_val=1)
            with dve.If(general > 0):
                dve.wait_ge(g_blocks_landed, 32)
                nc.vector.memset(zero, 0.0).then_inc(zero_ready, 1)
                for l in (1, 2):
                    q = S[l]
                    dve.sem_inc(q["acc_free"], FREE0)
                    STEPS = 4
                    with dve.Fori(0, TILES) as t:
                        done = [0]

                        def step(ins):
                            done[0] += 1
                            ins.then_inc(q["step"], 1)
                            dve.wait_ge(q["step"], t * STEPS + done[0])

                        if l == 2:
                            with dve.Fori(0, TURNS) as u:
                                for s in range(SLOTS):
                                    n = (t * TURNS + u) * SLOTS + s
                                    dve.wait_ge(q["adjT_ready"], n + (ADJT0 + 1))
                                    dve.wait_ge(q["adjT_used"], n + (USED0 - 1))
                                    nc.vector.tensor_scalar(posT[s % 2], adjT[s % 2], 0.0, None, ALU.is_gt)
                                    nc.vector.tensor_scalar(negT[s % 2], adjT[s % 2], 0.0, None, ALU.is_lt)\
                                        .then_inc(q["masks_ready"], 1)
                        dve.wait_ge(q["acc_ready"], t + 1)
                        if l == 1:
                            step(nc.vector.scalar_tensor_tensor(g_r[:, :], acc[0][:, 0:F], 1.0 - ALPHA, gX[:, t, :],
                                                                ALU.mult, ALU.add))
                            step(nc.vector.scalar_tensor_tensor(g_r[:, :], gH[:, t, :], ALPHA, g_r[:, :],
                                                                ALU.mult, ALU.add))
                        else:
                            for a in range(3):
                                last = nc.vector.tensor_copy(sums[:, a, :], acc[a][:, 0:F])
                            last.then_inc(q["sums_ready"], 1)
                            dve.wait_ge(q["sumsT_made"], t + 1)
                            nc.vector.tensor_copy(sumsT, tail[:, 0:3 * P].rearrange("p (a i) -> p a i", a=3))\
                                .then_inc(q["sumsT_ready"], 1)
                            dve.wait_ge(q["node_ready"], t + 1)
                            step(nc.vector.tensor_tensor(g_r[:, :], g_node[:, :], proj[:, F:2 * F], ALU.add))
                            step(nc.vector.tensor_tensor(g_r[:, :], g_r[:, :], gX1[:, t, :], ALU.add))
                        
                        step(nc.vector.bn_stats(g_stats[:, :], g_r[:, :]))
                        dve.sem_inc(wait_carrier, 1)
                        nc.vector.bn_aggr(g_mv[:, :], g_stats[:, :]).then_inc(q["var_ready"], 1)
                        dve.wait_ge(q["std_ready"], t + 1)
                        step(nc.vector.reciprocal(g_rstd[:, :], g_std[:, :]))
                        to = gX1 if l == 1 else gH
                        nc.vector.tensor_scalar(to[:, t, :], g_r[:, :], g_mv[:, 0:1], g_rstd[:, :], ALU.subtract, ALU.mult)\
                            .then_inc(q["tile_done"], 1)
                        dve.wait_ge(q["tile_done"], t + 1)
                        dve.sem_inc(q["acc_free"], 1)


_INS = ["x", "adj", "L0_gnn_h", "L1_gnn_node_weight", "L1_gnn_node_bias", "L1_gnn_edge_weight", "L1_gnn_edge_bias"]


def kernel(**inputs):
    import numpy as _np
    import concourse.bacc as _bacc
    from concourse import mybir as _mybir
    from concourse.bass_utils import run_bass_kernel_spmd as _run

    nc = _bacc.Bacc("TRN2", target_bir_lowering=False, num_devices=1)
    arrays, args = {}, []
    for name in _INS:
        a = _np.ascontiguousarray(inputs[name])
        arrays[f"in_{name}"] = a
        args.append(nc.dram_tensor(f"in_{name}", a.shape, _mybir.dt.from_np(a.dtype), kind="ExternalInput").ap())
    shape = inputs["x"].shape
    args.append(nc.dram_tensor("out_0", shape, _mybir.dt.float32, kind="ExternalOutput").ap())
    args.append(nc.dram_tensor("x1_rows", shape, _mybir.dt.float32, kind="Internal").ap())
    two_layer_graph_kernel(nc, *args)
    r = _run(nc, [arrays], core_ids=[0])
    return r.results[0]["out_0"]
```

```python
import concourse.bass as bass
from concourse import mybir
from contextlib import ExitStack


def two_layer_graph_kernel(nc, x, adj, h, wn, bn, we, be, out, x1_rows):
    fp32, bf16, fp16 = mybir.dt.float32, mybir.dt.bfloat16, mybir.dt.float16
    i32, u32 = mybir.dt.int32, mybir.dt.uint32
    ALU = mybir.AluOpType
    ACT = mybir.ActivationFunctionType
    AX = mybir.AxisListType

    P = 128
    N, F = x.shape
    ALPHA, EPS = 0.1, 1e-5
    TILES = N // P
    RING = 4
    RING2 = 8
    AHEAD = RING2 - 2
    SEG = 64
    SEGS = N // SEG
    K1 = 16
    K2 = 8
    BLOCKS = 3
    ITEMS = BLOCKS * P
    GATHERS = [BLOCKS, BLOCKS - 1] * (RING2 // 2)
    EDGES = (BLOCKS - 1) * P + P // 2
    PARTS = 4
    PW = N // PARTS
    LIFT = 2.0 ** 20
    LARGE = 3.0e38
    SEG_ROW, SEG_NO = range(2)
    FIELDS = 6
    COLUMN, ROW, VALUE = range(3)
    CW = 512
    CB = CW // P
    SLOTS = 4
    TURNS = N // CW // SLOTS

    x_blocks = x.rearrange("(b p) f -> p b f", p=P)
    h_blocks = h.rearrange("(b p) f -> p b f", p=P)
    x1_turns = x1_rows.rearrange("(u s p) f -> p u s f", s=RING, p=P)
    out_blocks = out.rearrange("(b p) f -> p b f", p=P)
    adj_tiles = adj.rearrange("(t p) c -> p t c", p=P)
    adj_segments = adj.rearrange("r (g c) -> (r g) c", c=SEG)
    adj_chunks = adj.rearrange("(t p) (u s c) -> p t u s c", p=P, s=SLOTS, c=CW)

    ctx = ExitStack()
    with ctx:
        def sb(name, shape, dt=fp32):
            return ctx.enter_context(nc.sbuf_tensor(name, shape, dt))

        def pair(name, shape, dt=fp32):
            return [sb(f"{name}{i}", shape, dt) for i in range(2)]

        def ring(name, shape, dt=fp32):
            return [sb(f"{name}{s}", shape, dt) for s in range(RING)]

        def sem(name):
            return ctx.enter_context(nc.semaphore(name))

        ident = sb("ident", [P, P])
        ones = sb("ones", [P, P])
        before = sb("before", [P, P])
        place_no = sb("place_no", [P, K1 + ITEMS], fp16)
        row_no = sb("row_no", [P, P])
        seg_no = sb("seg_no", [P, SEGS])
        my_row = sb("my_row", [P, K1])
        half = sb("half", [P, 2])
        base = sb("base", [P, 2])
        base_step = sb("base_step", [P, 2])
        eps = sb("eps", [P, 1])

        A = pair("adj", [P, N])
        space = sb("magnitudes", [P, N])
        mag = [space[:, i * (N // 2):(i + 1) * (N // 2)].bitcast(bf16) for i in range(2)]
        Wn = sb("Wn", [P, 2, F])[:, :, :]
        We = sb("We", [P, F])[:, :]
        bn_row = sb("bn_row", [1, F])[:, :]
        be_row = sb("be_row", [1, F])[:, :]
        diag = pair("diag", [P, P])
        discard = sb("discard", [P, P])
        discard2 = sb("discard2", [P, BLOCKS, SEG])
        seg_max = pair("seg_max", [P, SEGS])
        filled = sb("filled", [P, SEGS])
        rest = sb("rest", [P, SEGS])
        top = pair("top", [P, K1])
        held = pair("held", [P, K1])
        entry1 = pair("entry1_", [P, K1, 2], bf16)
        place1 = pair("place1_", [P, K1 + ITEMS], bf16)
        rec1 = pair("rec1_", [P, BLOCKS, 2])
        seg_at = pair("seg_at", [P, BLOCKS])
        seg_index = pair("seg_index", [P, BLOCKS], u32)
        own_col = pair("own_col", [P, BLOCKS])
        in_use = pair("in_use", [P, BLOCKS])
        segs = pair("segs", [P, BLOCKS, SEG])
        val = pair("val", [P, BLOCKS, K2])
        col = pair("col", [P, BLOCKS, K2], u32)
        held2 = pair("held2_", [P, BLOCKS, K2])
        not_own = pair("not_own", [P, BLOCKS, K2])
        held3 = pair("held3_", [P, BLOCKS, K2])
        left = pair("left", [P, BLOCKS, K2])
        entry2 = pair("entry2_", [P, BLOCKS, K2, FIELDS], bf16)
        place2 = pair("place2_", [P, BLOCKS, K2 + ITEMS], bf16)
        rec2 = pair("rec2_", [P, BLOCKS, FIELDS])
        edge = pair("edge", [P, BLOCKS, 3])
        edge_col = ring("edge_col", [P, BLOCKS], u32)
        edge_col2 = [sb(f"edge_col2_{s}", [P, BLOCKS], u32) for s in range(RING2)]
        edges = sb("edges", [P, TILES, BLOCKS, 3])
        diag_val = sb("diag_val", [P, TILES, 1])
        diag_pos = sb("diag_pos", [P, TILES, 1])
        deg = sb("deg", [P, TILES, 1])
        cnt = sb("cnt", [P, TILES, BLOCKS])
        largest = sb("largest", [P, TILES, 1])
        ends1 = sb("ends1", [P, TILES, 1])
        ends2 = sb("ends2", [P, TILES, BLOCKS])
        below = sb("below", [P, TILES, 1])
        G = ring("gathered", [P, BLOCKS, F])
        pick = pair("pick", [P, BLOCKS + 1, 2, P])
        X1 = sb("X1", [P, TILES, F])
        X1_turns = X1[:, :, :].rearrange("p (u s) f -> p u s f", s=RING)
        xt = ring("xt", [P, F])
        ht = ring("ht", [P, F])
        r = pair("r", [P, F])
        node = pair("node", [P, F])
        stats = pair("stats", [P, 6])
        mv = pair("mv", [P, 2])
        std = pair("std", [P, 1])
        rstd = pair("rstd", [P, 1])
        sumsT2 = [A[i][:, 0:2 * P].rearrange("p (a i) -> p a i", a=2) for i in range(2)]
        G2 = [space[:, s * BLOCKS * F:(s + 1) * BLOCKS * F].rearrange("p (b f) -> p b f", f=F) for s in range(RING2)]
        x1_tile = [A[i][:, 4 * P:5 * P] for i in range(2)]
        bad = sb("bad", [P, 8])
        bad_any = sb("bad_any", [P, 1])
        verdict = sb("verdict", [1, 1], i32)

        bank = [ctx.enter_context(nc.psum_tensor(f"bank{i}", [P, 512], fp32)) for i in range(8)]
        counts = bank[0:2]
        edge_counts = [bank[1][:, 8:8 + BLOCKS], bank[0][:, 8:8 + BLOCKS]]
        packed1 = bank[2:4]
        packed2 = bank[4:6]
        acc1 = bank[6:8]
        sums2 = bank[2:4]
        proj2 = bank[4:6]
        judged = bank[0]

        wait_carrier = sem("wait_carrier")
        const_ready = sem("const_ready")
        weights_landed = sem("weights_landed")
        adj_landed = [[sem(f"adj_landed{i}_{q}") for q in range(PARTS)] for i in range(2)]
        rows_landed = [sem(f"rows_landed{s}") for s in range(RING)]
        segs_gathered = [sem(f"segs_gathered{s}") for s in range(RING)]
        gathered = [sem(f"gathered{s}_1") for s in range(RING)]
        gathered2 = [sem(f"gathered{s}_2") for s in range(RING2)]
        x1_landed = sem("x1_landed")
        out_landed = sem("out_landed")
        (diag_apart, diag_ready, converted, folded, top_ready, counts1_ready, entry1_ready, place1_ready,
         packed1_ready, rec1_ready, edges_found, counts2_ready, entry2_ready, place2_ready,
         packed2_ready, rec2_ready, edge_ready, pick_ready, diag_pick_ready, acc_ready, var_ready, std_ready, x1_ready) = [
            sem(n) for n in
            ("diag_apart", "diag_ready", "converted", "folded", "top_ready", "counts1_ready", "entry1_ready",
             "place1_ready", "packed1_ready", "rec1_ready", "edges_found", "counts2_ready",
             "entry2_ready", "place2_ready", "packed2_ready", "rec2_ready", "edge_ready", "pick_ready", "diag_pick_ready",
             "acc_ready", "var_ready", "std_ready", "x1_ready")]
        (diag_step, fold_step, base_step_done, index_step, entry2_step, below_ready, edge_step,
         scan_step, found_step, norm_step, scale_step) = [
            sem(n) for n in
            ("diag_step", "fold_step", "base_step_done", "index_step", "entry2_step", "below_ready", "edge_step",
             "scan_step", "found_step", "norm_step", "scale_step")]
        (edge_col2_ready, x1_tile_ready, pick2_ready, sums2_ready, sumsT2_ready, proj2_ready, node_ready, var2_ready,
         std2_ready, result_ready, norm2_step, scale2_step) = [
            sem(n) for n in
            ("edge_col2_ready", "x1_tile_ready", "pick2_ready", "sums2_ready", "sumsT2_ready", "proj2_ready", "node_ready",
             "var2_ready", "std2_ready", "result_ready", "norm2_step", "scale2_step")]
        columns_ready = sem("columns_ready")
        place2_cleared = sem("place2_cleared")
        diag_pos_ready = sem("diag_pos_ready")
        verdict_step = sem("verdict_step")
        bad_ready = sem("bad_ready")
        judged_ready = sem("judged_ready")
        verdict_ready = sem("verdict_ready")

        def need(eng, s, value):
            if not isinstance(value, int) or value > 0:
                eng.wait_ge(s, value)

        def hold(eng, s, value):
            if not isinstance(value, int) or value > 0:
                eng.wait_ge(s, value)
                eng.sem_inc(wait_carrier, 1)

        def of(turn, j, lag, ring=RING):
            t = turn * ring + (j - lag)
            if isinstance(t, int) and not 0 <= t < TILES:
                return None
            return t, (j - lag) % ring, turn + (j - lag) // ring

        def steps(eng, step, lag, ahead=0, ring=RING):
            first, last = 8 // ring, TILES // ring - (1 if ahead else 0)
            for n in range(first * ring):
                step(n // ring, n % ring)
            with eng.Fori(first, last) as turn:
                for j in range(ring):
                    step(turn, j)
            for n in range(last * ring, TILES + lag):
                step(n // ring, n % ring)

        gX, gH = [A[a][:, :].rearrange("p (b f) -> p b f", f=F) for a in range(2)]
        gX1 = X1
        chunk = [space[:, a * CW:(a + 1) * CW] for a in range(SLOTS)]
        adjT, posT, negT = [[space[:, a * CW:(a + 1) * CW] for a in (SLOTS + m, SLOTS + m + 1)] for m in (0, 2, 4)]
        sums, sumsT = G[0][:, 0:3, :], G[1][:, 0:3, :]
        g_node, g_r, g_stats, g_mv, g_std, g_rstd = xt[0], r[0], stats[0], mv[0], std[0], rstd[0]
        tp, acc, tail, proj = bank[0:2], bank[2:5], bank[5], bank[6]
        zero = space[:, 12 * CW:12 * CW + P]
        zero_ready = sem("general_zero_ready")
        g_blocks_landed = sem("general_blocks_landed")
        g_out_landed = sem("general_out_landed")
        chunk_landed = {l: [sem(f"chunk_landed{l}_{s}") for s in range(SLOTS)] for l in (1, 2)}
        names = ["chunk_transposed", "adjT_ready", "adjT_used", "masks_ready",
                 "acc_ready", "acc_free", "sums_ready", "sumsT_made", "sumsT_ready", "proj_ready",
                 "node_ready", "var_ready", "std_ready", "tile_done", "step"]
        S = {l: {n: sem(f"general_{n}_{l}") for n in names} for l in (1, 2)}
        CHUNK0, ADJT0, USED0, FREE0 = SLOTS, 2, 2, 1

        block = ctx.enter_context(nc.Block())

        @block.sync
        def _(sp):
            def loads(turn, j):
                if now := of(turn, j, 0):
                    t, s, _ = now
                    i = s % 2
                    for q in range(PARTS):
                        hold(sp, converted, t * PARTS + (q + 1 - 2 * PARTS))
                        sp.dma_start(A[i][:, q * PW:(q + 1) * PW], adj_tiles[:, t, q * PW:(q + 1) * PW])\
                            .then_inc(adj_landed[i][q], 16)
                if now := of(turn, j, 3):
                    t, s, _ = now
                    hold(sp, var_ready, t - (RING - 1))
                    sp.dma_start(xt[s][:, :], x_blocks[:, t, :]).then_inc(rows_landed[s], 16)
                    sp.dma_start(ht[s][:, :], h_blocks[:, t, :]).then_inc(rows_landed[s], 16)

            steps(sp, loads, 3)
            sp.dma_start(Wn, wn.rearrange("(a p) f -> p a f", p=P)).then_inc(weights_landed, 16)
            sp.dma_start(We, we).then_inc(weights_landed, 16)
            sp.dma_start(bn_row, bn.rearrange("(a f) -> a f", a=1)).then_inc(weights_landed, 16)
            sp.dma_start(be_row, be.rearrange("(a f) -> a f", a=1)).then_inc(weights_landed, 16)
            with sp.Fori(0, TILES // RING) as u:
                hold(sp, x1_ready, u * RING + RING)
                sp.dma_start(x1_turns[:, u, :, :], X1_turns[:, u, :, :]).then_inc(x1_landed, 16)
            with sp.Fori(0, TILES) as t:
                hold(sp, result_ready, t + 1)
                sp.dma_start(out_blocks[:, t, :], X1[:, t, :]).then_inc(out_landed, 16)
            sp.wait_ge(out_landed, 16 * TILES)

            sp.wait_ge(verdict_ready, 1)
            general = sp.value_load(verdict[0:1, 0:1], min_val=0, max_val=1)
            with sp.If(general > 0):
                sp.dma_start(gX, x_blocks).then_inc(g_blocks_landed, 16)
                sp.dma_start(gH, h_blocks).then_inc(g_blocks_landed, 16)
                for l in (1, 2):
                    if l == 2:
                        sp.wait_ge(S[1]["chunk_transposed"], CHUNK0 + TILES * TURNS * SLOTS)
                    sp.sem_inc(S[l]["chunk_transposed"], CHUNK0)
                    with sp.Fori(0, TILES) as t:
                        with sp.Fori(0, TURNS) as u:
                            for s in range(SLOTS):
                                sp.wait_ge(S[l]["chunk_transposed"], (t * TURNS + u) * SLOTS + (s + 1))
                                sp.dma_start(chunk[s], adj_chunks[:, t, u, s, :]).then_inc(chunk_landed[l][s], 16)
                        if l == 2:
                            sp.wait_ge(S[2]["tile_done"], t + 1)
                            sp.dma_start(out_blocks[:, t, :], gH[:, t, :]).then_inc(g_out_landed, 16)
                sp.wait_ge(g_out_landed, 16 * TILES)

        @block.gpsimd
        def _(pool):
            gp = nc.gpsimd
            pool.memset(ident[:, :], 0.0).then_inc(const_ready, 1)
            pool.memset(ones[:, :], 1.0).then_inc(const_ready, 1)
            pool.memset(before[:, :], 1.0).then_inc(const_ready, 1)
            pool.memset(eps[:, :], EPS).then_inc(const_ready, 1)
            pool.memset(half[:, :], 1.0).then_inc(const_ready, 1)
            pool.memset(base[:, 0:1], float(-SEGS - 1)).then_inc(const_ready, 1)
            pool.memset(base[:, 1:2], float(SEG - 1)).then_inc(const_ready, 1)
            pool.memset(base_step[:, 0:1], float(P * SEGS)).then_inc(const_ready, 1)
            pool.memset(base_step[:, 1:2], float(P)).then_inc(const_ready, 1)
            for to, first, across in ((place_no, -K1, 0), (row_no, 1, 0), (seg_no, 1, 0)):
                pool.iota(to[:, :], [[1, to.shape[1]]], base=first, channel_multiplier=across,
                          allow_small_or_imprecise_dtypes=True).then_inc(const_ready, 1)
            pool.iota(my_row[:, :], [[0, K1]], base=1, channel_multiplier=1,
                      allow_small_or_imprecise_dtypes=True).then_inc(const_ready, 1)
            pool.wait_ge(const_ready, 13)
            pool.affine_select(out=ident[:, :], in_=ident[:, :], compare_op=ALU.not_equal, fill=1.0,
                               base=0, pattern=[[-1, P]], channel_multiplier=1).then_inc(const_ready, 1)
            pool.affine_select(out=before[:, :], in_=before[:, :], compare_op=ALU.is_gt, fill=0.0,
                               base=0, pattern=[[1, P]], channel_multiplier=-1).then_inc(const_ready, 1)
            for i, sign in ((0, -1), (1, 1)):
                pool.affine_select(out=half[:, i:i + 1], in_=half[:, i:i + 1], compare_op=ALU.is_gt, fill=0.0,
                                   base=P // 2 if i == 0 else 1 - P // 2, pattern=[[1, 1]],
                                   channel_multiplier=sign).then_inc(const_ready, 1)
            pool.wait_ge(const_ready, 17)

            def apart(t, s, own):
                i = s % 2
                for q in range(PARTS):
                    hold(pool, adj_landed[i][q], own * 32 + (s // 2 * 16 + 16))
                hold(pool, diag_ready, t - 1)
                own_block = A[i][:, :].rearrange("p (b c) -> p b c", c=P)[:, t, :]
                gp.tensor_tensor(diag[i][:, :], own_block, ident[:, :], ALU.mult).then_inc(diag_step, 1)
                hold(pool, diag_step, t + 1)
                gp.tensor_tensor(own_block, own_block, diag[i][:, :], ALU.subtract).then_inc(diag_apart, 1)

            def segment_entries(t, i):
                hold(pool, top_ready, t + 1)
                hold(pool, packed1_ready, t - 1)
                gp.tensor_tensor(entry1[i][:, :, SEG_ROW], my_row[:, :], held[i][:, :], ALU.mult)
                gp.tensor_copy(entry1[i][:, :, SEG_NO], top[i][:, :]).then_inc(entry1_ready, 1)

            def segment_gather(t, i, s):
                hold(pool, rec1_ready, t + 1)
                hold(pool, edges_found, t - 1)
                hold(pool, below_ready, t - 1)
                hold(pool, base_step_done, t)
                gp.tensor_scalar(seg_at[i][:, :], rec1[i][:, :, SEG_ROW], float(SEGS), base[:, 0:1], ALU.mult, ALU.add)
                gp.tensor_scalar(own_col[i][:, :], rec1[i][:, :, SEG_NO], float(-SEG), base[:, 1:2], ALU.mult, ALU.add)\
                    .then_inc(index_step, 1)
                gp.tensor_scalar(in_use[i][:, :], rec1[i][:, :, SEG_ROW], 0.0, None, ALU.is_gt)
                hold(pool, index_step, 3 * t + 1)
                gp.tensor_tensor(seg_at[i][:, :], seg_at[i][:, :], rec1[i][:, :, SEG_NO], ALU.add)\
                    .then_inc(index_step, 1)
                gp.tensor_tensor(own_col[i][:, :], own_col[i][:, :], rec1[i][:, :, SEG_ROW], ALU.add)
                gp.tensor_tensor(base[:, :], base[:, :], base_step[:, :], ALU.add).then_inc(base_step_done, 1)
                hold(pool, index_step, 3 * t + 2)
                gp.tensor_scalar(seg_index[i][:, :], seg_at[i][:, :], 0.0, None, ALU.max).then_inc(index_step, 1)
                hold(pool, index_step, 3 * t + 3)
                for b in range(BLOCKS):
                    gp.indirect_dma_start(
                        out=segs[i][:, b, :], out_offset=None, in_=adj_segments,
                        in_offset=bass.IndirectOffsetOnAxis(ap=seg_index[i][:, b:b + 1], axis=0),
                        bounds_check=N * SEGS - 1, oob_is_err=False).then_inc(segs_gathered[s], 16)

            def edge_gather(t, i, s):
                hold(pool, rec2_ready, t + 1)
                q, e = rec2[i], edge[i]
                gp.tensor_scalar(e[:, :, COLUMN], q[:, :, 1], float(SEG), float(-SEG), ALU.mult, ALU.add)
                gp.tensor_tensor(e[:, :, VALUE], q[:, :, 3], q[:, :, 4], ALU.add).then_inc(edge_step, 1)
                gp.tensor_copy(e[:, :, ROW], q[:, :, 0])
                hold(pool, edge_step, 2 * t + 1)
                gp.tensor_tensor(e[:, :, COLUMN], e[:, :, COLUMN], q[:, :, 2], ALU.add)
                gp.tensor_tensor(e[:, :, VALUE], e[:, :, VALUE], q[:, :, 5], ALU.add).then_inc(edge_step, 1)
                hold(pool, acc_ready, t - (RING - 1))
                hold(pool, edge_step, 2 * t + 2)
                gp.tensor_copy(edges[:, t, :, :], e[:, :, :])
                gp.tensor_scalar(edge_col[s][:, :], e[:, :, COLUMN], 0.0, None, ALU.max).then_inc(edge_ready, 1)
                hold(pool, edge_ready, t + 1)
                for b in range(BLOCKS):
                    gp.indirect_dma_start(
                        out=G[s][:, b, :], out_offset=None, in_=x,
                        in_offset=bass.IndirectOffsetOnAxis(ap=edge_col[s][:, b:b + 1], axis=0),
                        bounds_check=N - 1, oob_is_err=False).then_inc(gathered[s], 16)

            def layer1(turn, j):
                if now := of(turn, j, -1):
                    apart(*now)
                if now := of(turn, j, 1):
                    segment_gather(now[0], now[1] % 2, now[1])
                if now := of(turn, j, 3):
                    edge_gather(now[0], now[1] % 2, now[1])
                if now := of(turn, j, 0):
                    segment_entries(now[0], now[1] % 2)

            apart(0, 0, 0)
            steps(pool, layer1, 3, ahead=1)

            pool.wait_ge(edge_ready, TILES)
            column = edges[:, :, :, COLUMN]
            gp.tensor_scalar(column, column, 0.0, None, ALU.max).then_inc(columns_ready, 1)
            pool.wait_ge(columns_ready, 1)
            last_block = edges[:, :, BLOCKS - 1, COLUMN].rearrange("p (u i) -> p u i", i=2)
            gp.tensor_tensor(last_block[:, :, 0], last_block[:, :, 0], last_block[:, :, 1], ALU.add)\
                .then_inc(columns_ready, 1)

            def layer2(turn, j):
                t, s, _ = of(turn, j, 0, RING2)
                hold(pool, sums2_ready, t - (RING2 - 1))
                hold(pool, edge_col2_ready, t + 1)
                for b in range(GATHERS[s]):
                    if b == BLOCKS - 1:
                        hold(pool, sums2_ready, t - (RING2 - 2))
                    gp.indirect_dma_start(
                        out=G2[s][:, b, :], out_offset=None, in_=x1_rows,
                        in_offset=bass.IndirectOffsetOnAxis(ap=edge_col2[s][:, b:b + 1], axis=0),
                        bounds_check=N - 1, oob_is_err=False).then_inc(gathered2[s], 16)

            pool.wait_ge(x1_landed, 16 * (TILES // RING))
            steps(pool, layer2, 0, ring=RING2)

        @block.tensor
        def _(pe):
            pe.wait_ge(const_ready, 17)

            def segments_before(t, s):
                i = s % 2
                need(pe, top_ready, t + 1)
                nc.tensor.matmul(counts[i][:, 0:1], before[:, :], deg[:, t, :], start=True, stop=True)\
                    .then_inc(counts1_ready, 1)

            def edges_before(t, s):
                i = s % 2
                need(pe, edges_found, t + 1)
                nc.tensor.matmul(edge_counts[i], before[:, :], cnt[:, t, :], start=True, stop=False)
                for b in range(1, BLOCKS):
                    last = nc.tensor.matmul(edge_counts[i][:, b:BLOCKS], ones[:, :], cnt[:, t, 0:BLOCKS - b],
                                            start=False, stop=(b == BLOCKS - 1))
                last.then_inc(counts2_ready, 1)

            def segment_list(t, s):
                i = s % 2
                need(pe, place1_ready, t + 1)
                need(pe, entry1_ready, t + 1)
                need(pe, rec1_ready, t - 1)
                for b in range(BLOCKS):
                    for k in range(K1):
                        at = K1 - k + b * P
                        last = nc.tensor.matmul(packed1[i][:, 2 * b:2 * b + 2], place1[i][:, at:at + P],
                                                entry1[i][:, k, :], start=(k == 0), stop=(k == K1 - 1))
                last.then_inc(packed1_ready, 1)

            def edge_list(t, s):
                i = s % 2
                need(pe, place2_cleared, 2)
                need(pe, place2_ready, t + 1)
                need(pe, entry2_ready, t + 1)
                need(pe, rec2_ready, t - 1)
                for to in range(BLOCKS):
                    for b in range(BLOCKS):
                        for k in range(K2):
                            at = K2 - k + to * P - (P // 2 if to == BLOCKS - 1 and i == 1 else 0)
                            last = nc.tensor.matmul(packed2[i][:, FIELDS * to:FIELDS * (to + 1)],
                                                    place2[i][:, b, at:at + P], entry2[i][:, b, k, :],
                                                    start=(b == 0 and k == 0),
                                                    stop=(b == BLOCKS - 1 and k == K2 - 1))
                last.then_inc(packed2_ready, 1)

            def row_sums(t, s, own):
                i = s % 2
                need(pe, gathered[s], own * (16 * BLOCKS) + 16 * BLOCKS)
                need(pe, pick_ready, t + 1)
                need(pe, diag_pick_ready, t + 1)
                need(pe, rows_landed[s], own * 32 + 32)
                need(pe, var_ready, t - 1)
                for b in range(BLOCKS):
                    nc.tensor.matmul(acc1[i][:, 0:F], pick[i][:, b, 1, :], G[s][:, b, :],
                                     start=(b == 0), stop=False)
                nc.tensor.matmul(acc1[i][:, 0:F], pick[i][:, BLOCKS, 1, :], xt[s][:, :], start=False, stop=True)\
                    .then_inc(acc_ready, 1)

            def layer1(turn, j):
                if now := of(turn, j, 4):
                    row_sums(*now)
                if now := of(turn, j, 0):
                    segments_before(*now[:2])
                if now := of(turn, j, 2):
                    edges_before(*now[:2])
                if now := of(turn, j, 0):
                    segment_list(*now[:2])
                if now := of(turn, j, 2):
                    edge_list(*now[:2])

            steps(pe, layer1, 4)
            pe.wait_ge(bad_ready, 1)
            nc.tensor.matmul(judged[:, 0:1], ones[:, :], bad_any[:, :], start=True, stop=True).then_inc(judged_ready, 1)
            pe.wait_ge(weights_landed, 64)

            def layer2(turn, j):
                if now := of(turn, j, 0, RING2):
                    t, s, own = now
                    i = s % 2
                    need(pe, gathered2[s], own * (16 * GATHERS[s]) + 16 * GATHERS[s])
                    need(pe, x1_tile_ready, t + 1)
                    need(pe, pick2_ready, t + 1)
                    need(pe, sumsT2_ready, t - 1)
                    for b in range(BLOCKS):
                        rows = G2[s - i] if b == BLOCKS - 1 else G2[s]
                        nc.tensor.matmul(sums2[i][:, 0:2 * P], rows[:, b, :], pick[i][:, b, :, :],
                                         start=(b == 0), stop=False)
                    nc.tensor.matmul(sums2[i][:, 0:2 * P], x1_tile[i], pick[i][:, BLOCKS, :, :],
                                     start=False, stop=True).then_inc(sums2_ready, 1)
                if now := of(turn, j, 1, RING2):
                    t, s, _ = now
                    i = s % 2
                    need(pe, sumsT2_ready, t + 1)
                    need(pe, var2_ready, t - 1)
                    node, edge_out = proj2[i][:, 0:F], proj2[i][:, F:2 * F]
                    nc.tensor.matmul(node, sumsT2[i][:, 0, :], Wn[:, 0, :], start=True, stop=False)
                    nc.tensor.matmul(node, ones[0:1, :], bn_row, start=False, stop=True)
                    nc.tensor.matmul(edge_out, sumsT2[i][:, 1, :], We, start=True, stop=False)
                    nc.tensor.matmul(edge_out, ones[0:1, :], be_row, start=False, stop=True)\
                        .then_inc(proj2_ready, 1)

            steps(pe, layer2, 1, ring=RING2)

            pe.wait_ge(verdict_ready, 1)
            general = pe.value_load(verdict[0:1, 0:1], min_val=0, max_val=1)
            with pe.If(general > 0):
                pe.wait_ge(g_blocks_landed, 32)
                pe.wait_ge(zero_ready, 1)
                for l in (1, 2):
                    q = S[l]
                    rows = gX if l == 1 else gX1
                    if l == 2:
                        pe.wait_ge(S[1]["tile_done"], TILES)

                    def transposes(n, s, u_turn):
                        pe.wait_ge(chunk_landed[l][s], 16 * u_turn + 16)
                        pe.wait_ge(q["adjT_ready"], n + (ADJT0 - 1))
                        for b in range(CB):
                            last = nc.tensor.transpose(tp[s % 2][:, b * P:(b + 1) * P],
                                                       chunk[s][:, b * P:(b + 1) * P], ident[:, :])
                        last.then_inc(q["chunk_transposed"], 1)

                    def products(n, s, u):
                        pe.wait_ge(q["adjT_ready"], n + (ADJT0 + 1))
                        if l == 2:
                            pe.wait_ge(q["masks_ready"], n + 1)
                        parts = [adjT] if l == 1 else [adjT, posT, negT]
                        for b in range(CB):
                            for a, part in enumerate(parts):
                                last = nc.tensor.matmul(acc[a][:, 0:F], part[s % 2][:, b * P:(b + 1) * P],
                                                        rows[:, u * (SLOTS * CB) + (s * CB + b), :],
                                                        start=False, stop=False, skip_group_check=True)
                        last.then_inc(q["adjT_used"], 1)

                    with pe.Fori(0, TILES) as t:
                        pe.wait_ge(q["acc_free"], t + 1)
                        for a in range(1 if l == 1 else 3):
                            last = nc.tensor.matmul(acc[a][:, 0:F], zero, ident[:, :], start=True, stop=False,
                                             skip_group_check=True)
                        with pe.Fori(0, TURNS) as u:
                            turn = t * TURNS + u
                            n = turn * SLOTS
                            transposes(n, 0, turn)
                            for s in range(1, SLOTS):
                                transposes(n + s, s, turn)
                                products(n + (s - 1), s - 1, u)
                            products(n + (SLOTS - 1), SLOTS - 1, u)
                        for a in range(1 if l == 1 else 3):
                            last = nc.tensor.matmul(acc[a][:, 0:F], zero, ident[:, :], start=False, stop=True,
                                             skip_group_check=True)
                        last.then_inc(q["acc_ready"], 1)
                        if l == 2:
                            pe.wait_ge(q["sums_ready"], t + 1)
                            for a in range(3):
                                last = nc.tensor.transpose(tail[:, a * P:(a + 1) * P], sums[:, a, :], ident[:, :])
                            last.then_inc(q["sumsT_made"], 1)
                            pe.wait_ge(q["sumsT_ready"], t + 1)
                            nc.tensor.matmul(proj[:, 0:F], sumsT[:, 1, :], Wn[:, 0, :], start=True, stop=False)
                            nc.tensor.matmul(proj[:, 0:F], sumsT[:, 2, :], Wn[:, 1, :], start=False, stop=False)
                            nc.tensor.matmul(proj[:, 0:F], ones[0:1, :], bn_row, start=False, stop=True)
                            nc.tensor.matmul(proj[:, F:2 * F], sumsT[:, 0, :], We, start=True, stop=False)
                            nc.tensor.matmul(proj[:, F:2 * F], ones[0:1, :], be_row, start=False, stop=True)\
                                .then_inc(q["proj_ready"], 1)

        @block.scalar
        def _(act):
            act.wait_ge(const_ready, 17)

            def first_magnitudes(t, s, own):
                i = s % 2
                need(act, diag_apart, t + 1)
                need(act, diag_ready, t)
                nc.scalar.activation(discard[:, :], diag[i][:, :], ACT.Copy,
                                     accum_out=diag_val[:, t, :]).then_inc(diag_ready, 1)
                need(act, folded, t - 1)
                magnitudes(t, i, 0)

            def magnitudes(t, i, q):
                nc.scalar.activation(mag[i][:, q * PW:(q + 1) * PW], A[i][:, q * PW:(q + 1) * PW], ACT.Abs,
                                     scale=LIFT).then_inc(converted, 1)

            def diagonal_pick(t, s):
                i = s % 2
                need(act, acc_ready, t - 1)
                nc.scalar.activation(pick[i][:, BLOCKS, 1, :], ident[:, :], ACT.Copy, scale=diag_val[:, t, :])\
                    .then_inc(diag_pick_ready, 1)

            def entries_below_zero(t, s, own):
                i = s % 2
                need(act, segs_gathered[s], own * (16 * BLOCKS) + 16 * BLOCKS)
                need(act, below_ready, t)
                nc.scalar.activation(discard2[:, :, :], segs[i][:, :, :], ACT.Relu, scale=-LIFT,
                                     accum_out=below[:, t, :]).then_inc(below_ready, 1)

            def segment_records(t, s):
                i = s % 2
                need(act, packed1_ready, t + 1)
                need(act, entry2_ready, t - 1)
                nc.scalar.activation(rec1[i][:, :, :], packed1[i][:, 0:2 * BLOCKS].rearrange("p (b c) -> p b c", c=2),
                                     ACT.Copy).then_inc(rec1_ready, 1)

            def edge_records(t, s):
                i = s % 2
                need(act, packed2_ready, t + 1)
                need(act, edge_ready, t - 1)
                packed = packed2[i][:, 0:FIELDS * BLOCKS].rearrange("p (b c) -> p b c", c=FIELDS)
                nc.scalar.activation(rec2[i][:, 0:BLOCKS - 1, :], packed[:, 0:BLOCKS - 1, :], ACT.Copy)
                nc.scalar.activation(rec2[i][:, BLOCKS - 1, :], packed[:, BLOCKS - 1, :], ACT.Copy,
                                     scale=half[:, i:i + 1]).then_inc(rec2_ready, 1)

            def deviation(t, s):
                i = s % 2
                need(act, var_ready, t + 1)
                nc.scalar.activation(std[i][:, :], mv[i][:, 1:2], ACT.Sqrt, bias=eps[:, :]).then_inc(std_ready, 1)

            def layer1(turn, j):
                if now := of(turn, j, 1):
                    segment_records(*now[:2])
                if now := of(turn, j, -1):
                    first_magnitudes(*now)
                if now := of(turn, j, 3):
                    edge_records(*now[:2])
                if now := of(turn, j, -1):
                    for q in range(1, PARTS):
                        magnitudes(now[0], now[1] % 2, q)
                if now := of(turn, j, 2):
                    entries_below_zero(*now)
                if now := of(turn, j, 3):
                    diagonal_pick(*now[:2])
                if now := of(turn, j, 4):
                    deviation(*now[:2])

            first_magnitudes(0, 0, 0)
            for q in range(1, PARTS):
                magnitudes(0, 0, q)
            steps(act, layer1, 5, ahead=1)

            def edge_columns(t, s):
                need(act, sums2_ready, t - (RING2 - 1))
                nc.scalar.activation(edge_col2[s][:, :], edges[:, t, :, COLUMN], ACT.Copy).then_inc(edge_col2_ready, 1)

            def own_rows(t, s):
                i = s % 2
                need(act, sums2_ready, t - 1)
                nc.scalar.activation(x1_tile[i], X1[:, t, :], ACT.Copy)
                for kind, scale in enumerate((diag_pos, diag_val)):
                    last = nc.scalar.activation(pick[i][:, BLOCKS, kind, :], ident[:, :], ACT.Copy,
                                                scale=scale[:, t, :])
                last.then_inc(x1_tile_ready, 1)

            def sums_to_sbuf(t, s):
                i = s % 2
                need(act, sums2_ready, t + 1)
                nc.scalar.activation(sumsT2[i], sums2[i][:, 0:2 * P].rearrange("p (a i) -> p a i", a=2),
                                     ACT.Copy).then_inc(sumsT2_ready, 1)

            def node_part(t, s):
                i = s % 2
                need(act, proj2_ready, t + 1)
                need(act, var2_ready, t - 1)
                nc.scalar.activation(node[i][:, :], proj2[i][:, 0:F], ACT.Relu).then_inc(node_ready, 1)

            def deviation2(t, s):
                i = s % 2
                need(act, var2_ready, t + 1)
                nc.scalar.activation(std[i][:, :], mv[i][:, 1:2], ACT.Sqrt, bias=eps[:, :]).then_inc(std2_ready, 1)

            def layer2(turn, j):
                if now := of(turn, j, -AHEAD, RING2):
                    edge_columns(*now[:2])
                if now := of(turn, j, 1, RING2):
                    sums_to_sbuf(*now[:2])
                if now := of(turn, j, -1, RING2):
                    own_rows(*now[:2])
                if now := of(turn, j, 2, RING2):
                    node_part(*now[:2])
                if now := of(turn, j, 3, RING2):
                    deviation2(*now[:2])

            act.wait_ge(columns_ready, 2)
            act.wait_ge(acc_ready, TILES)
            for t in range(AHEAD):
                edge_columns(t, t)
            act.wait_ge(x1_ready, TILES)
            act.wait_ge(diag_pos_ready, 1)
            own_rows(0, 0)
            steps(act, layer2, 3, ahead=AHEAD, ring=RING2)

            act.wait_ge(verdict_ready, 1)
            general = act.value_load(verdict[0:1, 0:1], min_val=0, max_val=1)
            with act.If(general > 0):
                for l in (1, 2):
                    q = S[l]
                    act.sem_inc(q["adjT_ready"], ADJT0)
                    act.sem_inc(q["adjT_used"], USED0)
                    with act.Fori(0, TILES) as t:
                        with act.Fori(0, TURNS) as u:
                            for s in range(SLOTS):
                                n = (t * TURNS + u) * SLOTS + s
                                act.wait_ge(q["chunk_transposed"], n + (CHUNK0 + 1))
                                act.wait_ge(q["adjT_used"], n + (USED0 - 1))
                                nc.scalar.activation(adjT[s % 2], tp[s % 2][:, :], ACT.Copy)\
                                    .then_inc(q["adjT_ready"], 1)
                        if l == 2:
                            act.wait_ge(q["proj_ready"], t + 1)
                            nc.scalar.activation(g_node[:, :], proj[:, 0:F], ACT.Relu).then_inc(q["node_ready"], 1)
                        act.wait_ge(q["var_ready"], t + 1)
                        nc.scalar.activation(g_std[:, :], g_mv[:, 1:2], ACT.Sqrt, bias=eps[:, :]).then_inc(q["std_ready"], 1)

        @block.vector
        def _(dve):
            ve = nc.vector
            for i in range(2):
                ve.memset(place2[i][:, :, K2 + EDGES:], 0.0).then_inc(place2_cleared, 1)
            dve.wait_ge(const_ready, 17)
            FOLDS = 4

            def fold(t, s):
                i = s % 2
                need(dve, converted, t * PARTS + PARTS)
                by_segment = mag[i].rearrange("p (g c) -> p g c", c=SEG)
                width = SEG // 2
                for n in range(FOLDS):
                    if n:
                        need(dve, fold_step, FOLDS * t + n)
                    ve.tensor_tensor(by_segment[:, :, 0:width], by_segment[:, :, 0:width],
                                     by_segment[:, :, width:2 * width], ALU.max).then_inc(fold_step, 1)
                    width //= 2
                need(dve, fold_step, FOLDS * t + FOLDS)
                ve.tensor_reduce(seg_max[i][:, :], by_segment[:, :, 0:4], AX.X, ALU.max).then_inc(folded, 1)

            def filled_segments(t, s):
                i = s % 2
                need(dve, folded, t + 1)
                ve.scalar_tensor_tensor(filled[:, :], seg_max[i][:, :], 0.0, seg_no[:, :], ALU.is_gt, ALU.mult)\
                    .then_inc(scan_step, 1)

            def last_8(t, s):
                i = s % 2
                hold(dve, entry1_ready, t - 1)
                hold(dve, scan_step, 4 * t + 1)
                ve.max(top[i][:, 0:8], filled[:, :]).then_inc(scan_step, 1)

            def without_8(t, s):
                i = s % 2
                hold(dve, scan_step, 4 * t + 2)
                ve.match_replace(rest[:, :], top[i][:, 0:8], filled[:, :], 0.0).then_inc(scan_step, 1)

            def next_8(t, s):
                i = s % 2
                hold(dve, scan_step, 4 * t + 3)
                ve.max(top[i][:, 8:16], rest[:, :]).then_inc(scan_step, 1)

            def how_many(t, s):
                i = s % 2
                need(dve, scan_step, 4 * t + 4)
                ve.tensor_scalar(held[i][:, :], top[i][:, :], 0.0, 0.0, ALU.is_gt, ALU.add,
                                 accum_out=deg[:, t, :]).then_inc(top_ready, 1)

            def largest_8(t, s, own):
                i = s % 2
                hold(dve, segs_gathered[s], own * (16 * BLOCKS) + 16 * BLOCKS)
                for b in range(BLOCKS):
                    last = ve.max(val[i][:, b, :], segs[i][:, b, :])
                last.then_inc(found_step, 1)

            def where(t, s):
                i = s % 2
                hold(dve, found_step, 4 * t + 1)
                for b in range(BLOCKS):
                    last = ve.max_index(col[i][:, b, :], val[i][:, b, :], segs[i][:, b, :])
                last.then_inc(found_step, 1)
                ve.scalar_tensor_tensor(held2[i][:, :, :], val[i][:, :, :], 0.0,
                                        in_use[i][:, :].unsqueeze(2).to_broadcast([P, BLOCKS, K2]),
                                        ALU.is_gt, ALU.mult).then_inc(found_step, 1)

            def other_than_diagonal(t, s):
                i = s % 2
                need(dve, found_step, 4 * t + 2)
                ve.tensor_tensor(not_own[i][:, :, :], col[i][:, :, :],
                                 own_col[i][:, :].unsqueeze(2).to_broadcast([P, BLOCKS, K2]),
                                 ALU.not_equal).then_inc(found_step, 1)
                ve.tensor_reduce(largest[:, t, :], val[i][:, :, :], AX.XY, ALU.max)
                need(dve, found_step, 4 * t + 3)
                ve.tensor_reduce(cnt[:, t, :], held2[i][:, :, :], AX.X, ALU.add)

            def entries_held(t, s):
                i = s % 2
                need(dve, found_step, 4 * t + 4)
                ve.tensor_tensor(held3[i][:, :, :], held2[i][:, :, :], not_own[i][:, :, :], ALU.mult)\
                    .then_inc(edges_found, 1)

            def segment_places(t, s):
                i = s % 2
                need(dve, counts1_ready, t + 1)
                ve.tensor_tensor(ends1[:, t, :], counts[i][:, 0:1], deg[:, t, :], ALU.add)
                need(dve, packed1_ready, t - 1)
                ve.tensor_scalar(place1[i][:, :], place_no[:, :], counts[i][:, 0:1], None, ALU.is_equal)\
                    .then_inc(place1_ready, 1)

            def edge_entries(t, s):
                i = s % 2
                e = entry2[i]
                need(dve, edges_found, t + 1)
                ve.tensor_tensor(left[i][:, :, :], val[i][:, :, :], held3[i][:, :, :], ALU.mult).then_inc(entry2_step, 1)
                need(dve, packed2_ready, t - 1)
                for field in (SEG_ROW, SEG_NO):
                    ve.tensor_tensor(e[:, :, :, field], rec1[i][:, :, field:field + 1].to_broadcast([P, BLOCKS, K2]),
                                     held3[i][:, :, :], ALU.mult)
                ve.tensor_tensor(e[:, :, :, 2], col[i][:, :, :], held3[i][:, :, :], ALU.mult)

            def value_part(t, s, part):
                i = s % 2
                need(dve, entry2_step, 5 * t + (2 * part - 5))
                ve.tensor_copy(entry2[i][:, :, :, part], left[i][:, :, :]).then_inc(entry2_step if part < 5 else entry2_ready, 1)

            def value_left(t, s, part):
                i = s % 2
                need(dve, entry2_step, 5 * t + (2 * part - 4))
                ve.tensor_tensor(left[i][:, :, :], left[i][:, :, :], entry2[i][:, :, :, part], ALU.subtract)\
                    .then_inc(entry2_step, 1)

            def edge_places(t, s):
                i = s % 2
                need(dve, counts2_ready, t + 1)
                ve.tensor_tensor(ends2[:, t, :], edge_counts[i], cnt[:, t, :], ALU.add)
                need(dve, packed2_ready, t - 1)
                for b in range(BLOCKS):
                    last = ve.tensor_scalar(place2[i][:, b, 0:K2 + EDGES], place_no[:, K1 - K2:K1 + EDGES],
                                            edge_counts[i][:, b:b + 1], None, ALU.is_equal)
                last.then_inc(place2_ready, 1)

            def value_picks(t, s):
                i = s % 2
                need(dve, edge_ready, t + 1)
                need(dve, acc_ready, t - 1)
                for b in range(BLOCKS):
                    last = ve.tensor_scalar(pick[i][:, b, 1, :], row_no[:, :], edges[:, t, b, ROW:ROW + 1],
                                            edges[:, t, b, VALUE:VALUE + 1], ALU.is_equal, ALU.mult)
                last.then_inc(pick_ready, 1)

            def moments(t, s):
                i = s % 2
                need(dve, acc_ready, t + 1)
                ve.scalar_tensor_tensor(r[i][:, :], acc1[i][:, 0:F], 1.0 - ALPHA, xt[s][:, :],
                                        ALU.mult, ALU.add).then_inc(norm_step, 1)
                need(dve, norm_step, 3 * t + 1)
                ve.scalar_tensor_tensor(r[i][:, :], ht[s][:, :], ALPHA, r[i][:, :],
                                        ALU.mult, ALU.add).then_inc(norm_step, 1)
                need(dve, norm_step, 3 * t + 2)
                ve.bn_stats(stats[i][:, :], r[i][:, :]).then_inc(norm_step, 1)
                hold(dve, norm_step, 3 * t + 3)
                ve.bn_aggr(mv[i][:, :], stats[i][:, :]).then_inc(var_ready, 1)

            def scaled(t, s):
                i = s % 2
                need(dve, std_ready, t + 1)
                ve.reciprocal(rstd[i][:, :], std[i][:, :]).then_inc(scale_step, 1)
                need(dve, scale_step, t + 1)
                ve.tensor_scalar(X1[:, t, :], r[i][:, :], mv[i][:, 0:1], rstd[i][:, :],
                                 ALU.subtract, ALU.mult).then_inc(x1_ready, 1)

            def layer1(turn, j):
                new = of(turn, j, 0)
                old = of(turn, j, 2)
                if new:
                    fold(*new[:2])
                    filled_segments(*new[:2])
                if old:
                    largest_8(*old)
                if new:
                    last_8(*new[:2])
                if old:
                    where(*old[:2])
                if new:
                    without_8(*new[:2])
                if old:
                    other_than_diagonal(*old[:2])
                if new:
                    next_8(*new[:2])
                if old:
                    entries_held(*old[:2])
                if new:
                    how_many(*new[:2])
                if old:
                    edge_entries(*old[:2])
                if now := of(turn, j, 5):
                    scaled(*now[:2])
                if old:
                    value_part(*old[:2], 3)
                if now := of(turn, j, 4):
                    moments(*now[:2])
                if old:
                    value_left(*old[:2], 3)
                if new:
                    segment_places(*new[:2])
                if old:
                    value_part(*old[:2], 4)
                if now := of(turn, j, 3):
                    value_picks(*now[:2])
                if old:
                    value_left(*old[:2], 4)
                    edge_places(*old[:2])
                    value_part(*old[:2], 5)

            steps(dve, layer1, 5)

            dve.wait_ge(diag_ready, TILES)
            ve.tensor_scalar(diag_pos[:, :, 0], diag_val[:, :, 0], 0.0, None, ALU.is_gt).then_inc(diag_pos_ready, 1)
            def picks(t, s, blocks, kind):
                i = s % 2
                need(dve, sums2_ready, t - 1)
                for b in blocks:
                    row = edges[:, t, b, ROW:ROW + 1]
                    if kind == 0:
                        last = ve.tensor_scalar(pick[i][:, b, 0, :], row_no[:, :], row, None, ALU.is_equal)
                    else:
                        last = ve.tensor_scalar(pick[i][:, b, 1, :], row_no[:, :], row,
                                                edges[:, t, b, VALUE:VALUE + 1], ALU.is_equal, ALU.mult)
                if kind == 1 and BLOCKS - 1 in blocks:
                    last.then_inc(pick2_ready, 1)

            def with_x1(t, s):
                i = s % 2
                need(dve, node_ready, t + 1)
                ve.tensor_tensor(r[i][:, :], X1[:, t, :], proj2[i][:, F:2 * F], ALU.add).then_inc(norm2_step, 1)

            def with_node(t, s):
                i = s % 2
                need(dve, norm2_step, 3 * t + 1)
                ve.tensor_tensor(r[i][:, :], r[i][:, :], node[i][:, :], ALU.add).then_inc(norm2_step, 1)

            def statistics(t, s):
                i = s % 2
                need(dve, norm2_step, 3 * t + 2)
                ve.bn_stats(stats[i][:, :], r[i][:, :]).then_inc(norm2_step, 1)

            def moments2(t, s):
                i = s % 2
                hold(dve, norm2_step, 3 * t + 3)
                ve.bn_aggr(mv[i][:, :], stats[i][:, :]).then_inc(var2_ready, 1)

            def inverse_deviation(t, s):
                i = s % 2
                need(dve, std2_ready, t + 1)
                ve.reciprocal(rstd[i][:, :], std[i][:, :]).then_inc(scale2_step, 1)

            def scaled2(t, s):
                i = s % 2
                need(dve, scale2_step, t + 1)
                ve.tensor_scalar(X1[:, t, :], r[i][:, :], mv[i][:, 0:1], rstd[i][:, :],
                                 ALU.subtract, ALU.mult).then_inc(result_ready, 1)

            def layer2(turn, j):
                new = of(turn, j, -1, RING2)
                old = of(turn, j, 3, RING2)
                older = of(turn, j, 4, RING2)
                if old:
                    with_x1(*old[:2])
                if new:
                    picks(*new[:2], range(0, 1), 0)
                if older:
                    inverse_deviation(*older[:2])
                if old:
                    with_node(*old[:2])
                if new:
                    picks(*new[:2], range(1, BLOCKS), 0)
                if older:
                    scaled2(*older[:2])
                if old:
                    statistics(*old[:2])
                if new:
                    picks(*new[:2], range(0, BLOCKS), 1)
                if old:
                    moments2(*old[:2])

            picks(0, 0, range(BLOCKS), 0)
            picks(0, 0, range(BLOCKS), 1)
            dve.wait_ge(edges_found, TILES)
            dve.wait_ge(below_ready, TILES)
            everywhere = ALU.max
            ve.tensor_reduce(bad[:, 0:1], deg[:, :, 0], AX.X, everywhere)
            ve.tensor_reduce(bad[:, 1:2], largest[:, :, 0], AX.X, everywhere)
            ve.tensor_reduce(bad[:, 2:3], cnt[:, :, :], AX.XY, everywhere)
            ve.tensor_reduce(bad[:, 3:4], ends1[:, :, 0], AX.X, everywhere)
            ve.tensor_reduce(bad[:, 4:5], ends2[:, :, :], AX.XY, everywhere)
            ve.tensor_reduce(bad[:, 5:6], below[:, :, 0], AX.X, everywhere)
            ve.tensor_reduce(bad[:, 6:7], diag_val[:, :, 0], AX.X, ALU.min).then_inc(verdict_step, 1)
            dve.wait_ge(verdict_step, 1)
            ve.tensor_scalar(bad[:, 0:1], bad[:, 0:1], float(K1), None, ALU.is_ge)
            ve.tensor_scalar(bad[:, 1:2], bad[:, 1:2], LARGE, None, ALU.is_gt)
            ve.tensor_scalar(bad[:, 2:3], bad[:, 2:3], float(K2), None, ALU.is_ge)
            ve.tensor_scalar(bad[:, 3:4], bad[:, 3:4], float(ITEMS), None, ALU.is_gt)
            ve.tensor_scalar(bad[:, 4:5], bad[:, 4:5], float(EDGES), None, ALU.is_gt)
            ve.tensor_scalar(bad[:, 5:6], bad[:, 5:6], 0.0, None, ALU.not_equal)
            ve.tensor_scalar(bad[:, 6:7], bad[:, 6:7], 0.0, None, ALU.is_lt).then_inc(verdict_step, 1)
            dve.wait_ge(verdict_step, 2)
            ve.tensor_reduce(bad_any[:, :], bad[:, 0:7], AX.X, ALU.add).then_inc(bad_ready, 1)
            dve.wait_ge(judged_ready, 1)
            ve.tensor_scalar(verdict[:, :], judged[0:1, 0:1], 0.0, None, ALU.is_gt).then_inc(verdict_ready, 1)

            steps(dve, layer2, 4, ahead=1, ring=RING2)

            dve.wait_ge(verdict_ready, 1)
            general = dve.value_load(verdict[0:1, 0:1], min_val=0, max_val=1)
            with dve.If(general > 0):
                dve.wait_ge(g_blocks_landed, 32)
                nc.vector.memset(zero, 0.0).then_inc(zero_ready, 1)
                for l in (1, 2):
                    q = S[l]
                    dve.sem_inc(q["acc_free"], FREE0)
                    STEPS = 4
                    with dve.Fori(0, TILES) as t:
                        done = [0]

                        def step(ins):
                            done[0] += 1
                            ins.then_inc(q["step"], 1)
                            dve.wait_ge(q["step"], t * STEPS + done[0])

                        if l == 2:
                            with dve.Fori(0, TURNS) as u:
                                for s in range(SLOTS):
                                    n = (t * TURNS + u) * SLOTS + s
                                    dve.wait_ge(q["adjT_ready"], n + (ADJT0 + 1))
                                    dve.wait_ge(q["adjT_used"], n + (USED0 - 1))
                                    nc.vector.tensor_scalar(posT[s % 2], adjT[s % 2], 0.0, None, ALU.is_gt)
                                    nc.vector.tensor_scalar(negT[s % 2], adjT[s % 2], 0.0, None, ALU.is_lt)\
                                        .then_inc(q["masks_ready"], 1)
                        dve.wait_ge(q["acc_ready"], t + 1)
                        if l == 1:
                            step(nc.vector.scalar_tensor_tensor(g_r[:, :], acc[0][:, 0:F], 1.0 - ALPHA, gX[:, t, :],
                                                                ALU.mult, ALU.add))
                            step(nc.vector.scalar_tensor_tensor(g_r[:, :], gH[:, t, :], ALPHA, g_r[:, :],
                                                                ALU.mult, ALU.add))
                        else:
                            for a in range(3):
                                last = nc.vector.tensor_copy(sums[:, a, :], acc[a][:, 0:F])
                            last.then_inc(q["sums_ready"], 1)
                            dve.wait_ge(q["sumsT_made"], t + 1)
                            nc.vector.tensor_copy(sumsT, tail[:, 0:3 * P].rearrange("p (a i) -> p a i", a=3))\
                                .then_inc(q["sumsT_ready"], 1)
                            dve.wait_ge(q["node_ready"], t + 1)
                            step(nc.vector.tensor_tensor(g_r[:, :], g_node[:, :], proj[:, F:2 * F], ALU.add))
                            step(nc.vector.tensor_tensor(g_r[:, :], g_r[:, :], gX1[:, t, :], ALU.add))

                        step(nc.vector.bn_stats(g_stats[:, :], g_r[:, :]))
                        dve.sem_inc(wait_carrier, 1)
                        nc.vector.bn_aggr(g_mv[:, :], g_stats[:, :]).then_inc(q["var_ready"], 1)
                        dve.wait_ge(q["std_ready"], t + 1)
                        step(nc.vector.reciprocal(g_rstd[:, :], g_std[:, :]))
                        to = gX1 if l == 1 else gH
                        nc.vector.tensor_scalar(to[:, t, :], g_r[:, :], g_mv[:, 0:1], g_rstd[:, :], ALU.subtract, ALU.mult)\
                            .then_inc(q["tile_done"], 1)
                        dve.wait_ge(q["tile_done"], t + 1)
                        dve.sem_inc(q["acc_free"], 1)


_INS = ["x", "adj", "L0_gnn_h", "L1_gnn_node_weight", "L1_gnn_node_bias", "L1_gnn_edge_weight", "L1_gnn_edge_bias"]


def kernel(**inputs):
    import numpy as _np
    import concourse.bacc as _bacc
    from concourse import mybir as _mybir
    from concourse.bass_utils import run_bass_kernel_spmd as _run

    nc = _bacc.Bacc("TRN2", target_bir_lowering=False, num_devices=1)
    arrays, args = {}, []
    for name in _INS:
        a = _np.ascontiguousarray(inputs[name])
        arrays[f"in_{name}"] = a
        args.append(nc.dram_tensor(f"in_{name}", a.shape, _mybir.dt.from_np(a.dtype), kind="ExternalInput").ap())
    shape = inputs["x"].shape
    args.append(nc.dram_tensor("out_0", shape, _mybir.dt.float32, kind="ExternalOutput").ap())
    args.append(nc.dram_tensor("x1_rows", shape, _mybir.dt.float32, kind="Internal").ap())
    two_layer_graph_kernel(nc, *args)
    r = _run(nc, [arrays], core_ids=[0])
    return r.results[0]["out_0"]
```
